# Optimizing a Trainium2 kernel written in Bass

```python
import numpy as np
import jax
import jax.numpy as jnp

def _softmax(x, axis=-1):
    return jax.nn.softmax(x, axis=axis)

def _gelu(x):
    return jax.nn.gelu(x, approximate=True)

def _silu(x):
    return jax.nn.silu(x)

def _sigmoid(x):
    return jax.nn.sigmoid(x)

def _layernorm(x, axis=-1, eps=1e-05):
    m = jnp.mean(x, axis=axis, keepdims=True)
    v = jnp.var(x, axis=axis, keepdims=True)
    return (x - m) / jnp.sqrt(v + eps)

def _scatter_add(tgt, idx, src, axis=0):
    return tgt.at[idx].add(src)

def _segment_sum(src, seg, n):
    return jax.ops.segment_sum(src, seg, n)
kernel_name = 'mk_macaron_d1_jaxref_r8_b28879'

def setup_inputs(seed: int=0):
    np.random.seed(seed)
    _w = jnp.asarray

    def _L0_attn_setup():
        import jax, jax.numpy as jnp
        import numpy as np
        D_MODEL = 256
        D_HEAD = 128
        N_HEADS = 16
        D_LATENT = 64
        B = 2
        S = 256
        key = jax.random.key(seed)
        ks = jax.random.split(key, 6)
        sc = 0.02
        return {'x': jax.random.normal(ks[0], (B, S, D_MODEL), jnp.float32), 'W_down': jax.random.normal(ks[1], (D_LATENT, D_MODEL), jnp.float32) * sc, 'W_uk': jax.random.normal(ks[2], (N_HEADS * D_HEAD, D_LATENT), jnp.float32) * sc, 'W_uv': jax.random.normal(ks[3], (N_HEADS * D_HEAD, D_LATENT), jnp.float32) * sc, 'W_q': jax.random.normal(ks[4], (N_HEADS * D_HEAD, D_MODEL), jnp.float32) * sc, 'W_o': jax.random.normal(ks[5], (D_MODEL, N_HEADS * D_HEAD), jnp.float32) * sc}
    _L0_attn_in = _L0_attn_setup()

    def _L0_ffn_setup():
        import jax, jax.numpy as jnp
        import numpy as np
        import math
        NUM_EXPERTS = 12
        TOP_K = 2
        CAP_FACTOR = 1.25
        key = jax.random.key(seed)
        k0, k1, k2, k3, k4 = jax.random.split(key, 5)
        B, S, H, F = (4, 512, 256, 32)
        hidden_states = jax.random.normal(k0, (B, S, H), jnp.float32)
        gate_w = jax.random.normal(k1, (NUM_EXPERTS, H), jnp.float32) * 0.02
        w1 = jax.random.normal(k2, (NUM_EXPERTS, F, H), jnp.float32) * 0.02
        w2 = jax.random.normal(k3, (NUM_EXPERTS, H, F), jnp.float32) * 0.02
        w3 = jax.random.normal(k4, (NUM_EXPERTS, F, H), jnp.float32) * 0.02
        return dict(hidden_states=hidden_states, gate_w=gate_w, w1=w1, w2=w2, w3=w3)
    _L0_ffn_in = _L0_ffn_setup()
    _d = {'L0_attn_x': _L0_attn_in['x'], 'L0_attn_W_down': _L0_attn_in['W_down'], 'L0_attn_W_uk': _L0_attn_in['W_uk'], 'L0_attn_W_uv': _L0_attn_in['W_uv'], 'L0_attn_W_q': _L0_attn_in['W_q'], 'L0_attn_W_o': _L0_attn_in['W_o'], 'L0_ffn_gate_w': _L0_ffn_in['gate_w'], 'L0_ffn_w1': _L0_ffn_in['w1'], 'L0_ffn_w2': _L0_ffn_in['w2'], 'L0_ffn_w3': _L0_ffn_in['w3']}
    _x0 = _d['L0_attn_x']
    _d['L0_attn_x'] = jax.random.normal(jax.random.fold_in(jax.random.key(seed), 1), (2, 512, 256), dtype=_x0.dtype)
    del _x0
    return _d

def reference(L0_attn_x, L0_attn_W_down, L0_attn_W_uk, L0_attn_W_uv, L0_attn_W_q, L0_attn_W_o, L0_ffn_gate_w, L0_ffn_w1, L0_ffn_w2, L0_ffn_w3):

    def _L0_attn_ref(x, W_down, W_uk, W_uv, W_q, W_o):
        import jax, jax.numpy as jnp
        import numpy as np
        D_MODEL = 256
        D_HEAD = 128
        N_HEADS = 16
        D_LATENT = 64
        B = 2
        S = 256
        b, s, _ = x.shape
        h, dh = (N_HEADS, D_HEAD)
        latents = x @ W_down.T
        keys = latents @ W_uk.T
        values = latents @ W_uv.T
        q = (x @ W_q.T).reshape(b, s, h, dh).transpose(0, 2, 1, 3)
        k = keys.reshape(b, s, h, dh).transpose(0, 2, 1, 3)
        v = values.reshape(b, s, h, dh).transpose(0, 2, 1, 3)
        scores = jnp.einsum('bhqd,bhkd->bhqk', q, k) / jnp.sqrt(jnp.float32(dh))
        causal = jnp.tril(jnp.ones((s, s), dtype=bool))
        scores = jnp.where(causal, scores, -jnp.inf)
        attn = jax.nn.softmax(scores, axis=-1)
        ctx = jnp.einsum('bhqk,bhkd->bhqd', attn, v)
        ctx = ctx.transpose(0, 2, 1, 3).reshape(b, s, h * dh)
        return ctx @ W_o.T

    def _L0_ffn_ref(hidden_states, gate_w, w1, w2, w3):
        import jax, jax.numpy as jnp
        import numpy as np
        import math
        NUM_EXPERTS = 12
        TOP_K = 2
        CAP_FACTOR = 1.25
        B, S, H = hidden_states.shape
        T = B * S
        E = gate_w.shape[0]
        cap = math.ceil(T / E * CAP_FACTOR)
        x = hidden_states.reshape(T, H)
        logits = x @ gate_w.T
        probs = jax.nn.softmax(logits, axis=-1)
        rw, sel = jax.lax.top_k(probs, TOP_K)
        rw = rw / rw.sum(axis=-1, keepdims=True)
        ar_cap = jnp.arange(cap)
        ar_flat = jnp.arange(TOP_K * T, dtype=jnp.int32)

        def per_expert(e, we1, we2, we3):
            mask = sel.T == e
            fm = mask.ravel()
            pos = jnp.cumsum(fm) - 1
            slot_idx = jnp.where(fm & (pos < cap), pos, cap)
            buf = jnp.zeros(cap + 1, jnp.int32).at[slot_idx].set(ar_flat)
            flat = buf[:cap]
            valid = ar_cap < fm.sum()
            tok = flat % T
            slot = flat // T
            xs = x[tok]
            h = jax.nn.silu(xs @ we1.T * (xs @ we3.T)) @ we2.T
            w = jnp.where(valid, rw[tok, slot], 0.0)
            return (tok, h * w[:, None])
        toks, contribs = jax.vmap(per_expert)(jnp.arange(E), w1, w2, w3)
        out = jnp.zeros((T, H), x.dtype).at[toks.ravel()].add(contribs.reshape(-1, H))
        return out.reshape(B, S, H)
    x = L0_attn_x
    x = x + 0.5 * _L0_ffn_ref(_layernorm(x, axis=-1), L0_ffn_gate_w, L0_ffn_w1, L0_ffn_w2, L0_ffn_w3)
    x = x + _L0_attn_ref(_layernorm(x, axis=-1), L0_attn_W_down, L0_attn_W_uk, L0_attn_W_uv, L0_attn_W_q, L0_attn_W_o)
    x = x + 0.5 * _L0_ffn_ref(_layernorm(x, axis=-1), L0_ffn_gate_w, L0_ffn_w1, L0_ffn_w2, L0_ffn_w3)
    return x

_drawn_inputs = setup_inputs


def setup_inputs(seed=0):
    import zlib

    import numpy as np

    out = dict(_drawn_inputs(seed))
    spreads = {}
    factors = {'L0_attn_W_down': 7.206,
     'L0_attn_W_uk': 8.0,
     'L0_attn_W_uv': 6.324,
     'L0_attn_W_q': 8.0,
     'L0_attn_W_o': 6.436,
     'L0_ffn_gate_w': 8.0,
     'L0_ffn_w1': 8.0,
     'L0_ffn_w2': 8.0,
     'L0_ffn_w3': 8.0}
    for name, (base, spread) in spreads.items():
        noise = np.random.default_rng([zlib.crc32(name.encode()), seed]).standard_normal(out[name].shape)
        drawn = base * np.exp(spread * noise) if base else spread * noise
        out[name] = jnp.asarray(drawn.astype(out[name].dtype))
    for name, factor in factors.items():
        out[name] = (out[name] * factor).astype(out[name].dtype)
    return out
```

```python
import concourse.bass as bass
from concourse import mybir
from contextlib import ExitStack


def bass_macaron_moe_mla_moe(
    nc: bass.Bass,
    x_in: bass.AP,
    W_down: bass.AP,
    W_uk: bass.AP,
    W_uv: bass.AP,
    W_q: bass.AP,
    W_o: bass.AP,
    gate_w: bass.AP,
    w1: bass.AP,
    w2: bass.AP,
    w3: bass.AP,
    out: bass.AP,
):
    F32 = mybir.dt.float32
    BF16 = mybir.dt.bfloat16
    I32 = mybir.dt.int32
    ALU = mybir.AluOpType
    ACT = mybir.ActivationFunctionType
    AX = mybir.AxisListType

    P = 128
    B, SEQ, D = x_in.shape
    T = B * SEQ
    NB = T // P
    SB = SEQ // P
    DC = D // P
    HALF = T // 2
    HB = HALF // P
    E, F, _ = w1.shape
    EF = E * F
    FC = EF // P
    EPC = P // F
    CAP = -(-T * 5 // (E * 4))
    LAT = W_down.shape[0]
    H = W_uk.shape[0] // P
    NP = H // 2
    SCALE = 1.0 / float(P) ** 0.5
    EPS = 1e-5
    HUGE = 3.0e38
    UNITS = B * SB

    x_d = x_in.rearrange("b s d -> (b s) d").rearrange("(n p) d -> p n d", p=P)
    out_d = out.rearrange("b s d -> (b s) d").rearrange("(n p) d -> p n d", p=P)

    ctx = ExitStack()
    with ctx:
        def sb(name, shape, dt):
            return ctx.enter_context(nc.sbuf_tensor(name, shape, dt))

        def sem(name):
            return ctx.enter_context(nc.semaphore(name))

        ident = sb("ident", [P, P], F32)
        identb = sb("identb", [P, P], BF16)
        tri = sb("tri", [P, P], BF16)
        onesb = sb("onesb", [P, P], BF16)
        maskneg = sb("maskneg", [P, P], BF16)
        rank_i = sb("rank_i", [P, NB, E], I32)
        rank = sb("rank", [P, NB, E], F32)
        sel = sb("sel", [2 * E, FC, P], BF16)

        X = sb("X", [P, NB, D], F32)
        xn = sb("xn", [P, NB, D], F32)
        xT = sb("xT", [P, DC, T], F32)
        xT_hi = sb("xT_hi", [P, DC, T], BF16)
        xT_lo = sb("xT_lo", [P, DC, T], BF16)
        st = sb("st", [P, NB, 6], F32)
        mv = sb("mv", [P, NB, 2], F32)
        ve = sb("ve", [P, NB], F32)
        std = sb("std", [P, NB], F32)
        rstd = sb("rstd", [P, NB], F32)

        ffn_buf = sb("ffn_buf", [P, 4, T], F32)
        g = ffn_buf[:, 0:FC, :]
        h1c = ffn_buf[:, FC, :].rearrange("p (b n) -> p b n", b=2)
        hT_hi = sb("hT_hi", [P, FC, T], BF16)
        hT_lo = sb("hT_lo", [P, FC, T], BF16)
        lg = sb("lg", [P, NB, E], F32)
        eq = sb("eq", [P, NB, E], F32)
        tb = sb("tb", [P, NB, E], F32)
        cp = sb("cp", [P, NB, E], F32)
        l2 = sb("l2", [P, NB, E], F32)
        top = sb("top", [P, 2, NB], F32)
        tr = sb("tr", [P, 2, NB], F32)
        dlt = sb("dlt", [P, NB], F32)
        e2 = sb("e2", [P, NB], F32)
        den = sb("den", [P, NB], F32)
        rec = sb("rec", [P, NB], F32)
        rw = sb("rw", [P, 2, NB], F32)
        chosen = sb("chosen", [P, 2, NB, E], BF16)
        kept = sb("kept", [P, 2, NB, E], F32)
        wgt = sb("wgt", [P, NB, E], F32)
        wgt_hl = sb("wgt_hl", [P, NB, 2, E], BF16)
        wgtT = sb("wgtT", [2 * E, T], BF16)

        w1n = sb("w1n", [P, FC, D], F32)
        w3n = sb("w3n", [P, FC, D], F32)
        w2n = sb("w2n", [P, DC, EF], F32)
        gaten = sb("gaten", [E, D], F32)
        wdn = sb("wdn", [LAT, D], F32)
        gateT = sb("gateT", [P, DC, E], F32)
        w1T = [sb("w1T_hi", [P, DC, EF], BF16), sb("w1T_lo", [P, DC, EF], BF16)]
        w3T = [sb("w3T_hi", [P, DC, EF], BF16), sb("w3T_lo", [P, DC, EF], BF16)]
        w2T = [sb("w2T_hi", [P, FC, D], BF16), sb("w2T_lo", [P, FC, D], BF16)]
        wdT = [sb("wdT_hi", [P, DC, 2, LAT], BF16), sb("wdT_lo", [P, DC, 2, LAT], BF16)]
        wuk = sb("wuk", [P, H, LAT], F32)
        wuv = sb("wuv", [P, H, LAT], F32)
        wqo = sb("wqo", [P, 2, H * D], F32)
        wq = wqo[:, 0, :].rearrange("p (h d) -> p h d", h=H)
        wo = wqo[:, 1, :].rearrange("p (c n) -> p c n", c=DC)
        uc = wqo[:, :, :].rearrange("p a n -> p (a n)").bitcast(BF16).rearrange("p (h t) -> p h t", h=H)
        woT_buf = sb("woT_buf", [P, H * D], F32)
        woT = woT_buf[:, :].rearrange("p (h d) -> p h d", h=H)
        c_hi = woT_buf[:, :].bitcast(BF16).rearrange("p (n c) -> p n c", n=NB)
        c_lo = ffn_buf[:, :, :].rearrange("p a n -> p (a n)").bitcast(BF16).rearrange("p (n c) -> p n c", n=NB)
        Mq = [sb("Mq_hi", [P, DC, H, LAT], BF16), sb("Mq_lo", [P, DC, H, LAT], BF16)]
        Nv = [sb("Nv_hi", [P, NP, D], BF16), sb("Nv_lo", [P, NP, D], BF16)]

        latT_hi = sb("latT_hi", [P, T], BF16)
        latT_lo = sb("latT_lo", [P, T], BF16)
        lat = sb("lat", [P, NB, 2 * LAT + 1], BF16)
        stage = sb("stage", [P, 2, 2, T], BF16)
        prob = sb("prob", [P, 4, SEQ], F32)
        pT_hi = sb("pT_hi", [P, 2, SEQ], BF16)
        pT_lo = sb("pT_lo", [P, 2, SEQ], BF16)
        nmax = sb("nmax", [P, UNITS], F32)
        rsum = sb("rsum", [P, B, SB], F32)
        cst = sb("cst", [P, B, SB, LAT], F32)

        bank = [ctx.enter_context(nc.psum_tensor(f"bank{i}", [P, 512], F32)) for i in range(8)]

        ld = {n: sem(f"ld_{n}") for n in ("x0", "x1", "gate", "w1", "w3", "w2", "wd", "wq", "wuk", "wuv", "wo")}
        consts = sem("consts")
        const_step = sem("const_step")
        var_ready = [sem(f"var_ready{i}") for i in range(3)]
        std_ready = [sem(f"std_ready{i}") for i in range(3)]
        xn_ready = [sem(f"xn_ready{i}") for i in range(3)]
        xT_ps = [sem(f"xT_ps{i}") for i in range(3)]
        xT_32 = [sem(f"xT_32_{i}") for i in range(2)]
        xThi_ready = [sem(f"xThi_ready{i}") for i in range(3)]
        xTlo_ready = [sem(f"xTlo_ready{i}") for i in range(3)]
        lg_ps = [sem(f"lg_ps{i}") for i in range(2)]
        dlt_ready = [sem(f"dlt_ready{i}") for i in range(2)]
        e2_ready = [sem(f"e2_ready{i}") for i in range(2)]
        pos_ps = [sem(f"pos_ps{i}") for i in range(2)]
        wgt_ready = [sem(f"wgt_ready{i}") for i in range(2)]
        wgtT_ps = [sem(f"wgtT_ps{i}") for i in range(2)]
        wgtT_ready = [sem(f"wgtT_ready{i}") for i in range(2)]
        h_ps = [sem(f"h_ps{i}") for i in range(2)]
        h1_ready = [sem(f"h1_ready{i}") for i in range(2)]
        z_ready = [sem(f"z_ready{i}") for i in range(2)]
        silu_ready = [sem(f"silu_ready{i}") for i in range(2)]
        wexp_ps = [sem(f"wexp_ps{i}") for i in range(2)]
        hw_ready = [sem(f"hw_ready{i}") for i in range(2)]
        hThi_ready = [sem(f"hThi_ready{i}") for i in range(2)]
        hTlo_ready = [sem(f"hTlo_ready{i}") for i in range(2)]
        y_ps = [sem(f"y_ps{i}") for i in range(2)]
        x_added = [sem(f"x_added{i}") for i in range(3)]
        w_ps = sem("w_ps")
        w_hi = sem("w_hi")
        w_lo = sem("w_lo")
        m_ps = sem("m_ps")
        m_hi = sem("m_hi")
        m_lo = sem("m_lo")
        woT_ps = sem("woT_ps")
        woT_ready = sem("woT_ready")
        n_ps = sem("n_ps")
        n_hi = sem("n_hi")
        n_lo = sem("n_lo")
        lat_ps = sem("lat_ps")
        lat_hi = sem("lat_hi")
        lat_lo = sem("lat_lo")
        u_ps = sem("u_ps")
        u_hi = sem("u_hi")
        u_lo = sem("u_lo")
        u_moved = [sem("u_moved0"), sem("u_moved1")]
        s_ps = sem("s_ps")
        max_ready = sem("max_ready")
        prob_ready = sem("prob_ready")
        pT_ps = sem("pT_ps")
        pThi_ready = sem("pThi_ready")
        pTlo_ready = sem("pTlo_ready")
        ctx_ps = sem("ctx_ps")
        rsum_ready = sem("rsum_ready")
        ctx_free = sem("ctx_free")
        chi_ready = sem("chi_ready")
        clo_ready = sem("clo_ready")
        cT_ps = sem("cT_ps")
        cThi_ready = sem("cThi_ready")
        cTlo_ready = sem("cTlo_ready")
        attn_ps = sem("attn_ps")
        stored = sem("stored")
        dve_step = sem("dve_step")

        block = ctx.enter_context(nc.Block())

        def weight_splits():
            for n, wT in enumerate((w1T, w3T)):
                for c in range(DC):
                    yield bank[2 * n + c][:, 0:EF], [t[:, c, :] for t in wT]
            yield bank[4][:, 0:2 * D], [t[:, 0:2, :].rearrange("p j d -> p (j d)") for t in w2T]
            yield bank[5][:, 0:D], [t[:, 2, :] for t in w2T]
            src = bank[6][:, P:P + DC * LAT].rearrange("p (c l) -> p c l", c=DC)
            yield src.unsqueeze(2).to_broadcast([P, DC, 2, LAT]), [t[:, :, :, :] for t in wdT]
        N_W = 2 * DC + 3

        def tokens(t):
            return slice(t * HALF, (t + 1) * HALF)

        def blk(n):
            return slice(n * P, (n + 1) * P)

        @block.sync
        def _(sp):
            sp.dma_start(X[:, 0:HB, :], x_d[:, 0:HB, :]).then_inc(ld["x0"], 16)
            sp.dma_start(X[:, HB:NB, :], x_d[:, HB:NB, :]).then_inc(ld["x1"], 16)
            sp.dma_start(gaten[:, :], gate_w).then_inc(ld["gate"], 16)
            sp.dma_start(w1n[:, :, :], w1.rearrange("e f d -> (e f) d").rearrange("(j p) d -> p j d", p=P)).then_inc(ld["w1"], 16)
            sp.dma_start(w3n[:, :, :], w3.rearrange("e f d -> (e f) d").rearrange("(j p) d -> p j d", p=P)).then_inc(ld["w3"], 16)
            for c in range(DC):
                sp.dma_start(w2n[:, c, :].rearrange("p (e f) -> p e f", e=E),
                             w2[:, blk(c), :].rearrange("e p f -> p e f")).then_inc(ld["w2"], 16)
            sp.dma_start(wdn[:, :], W_down).then_inc(ld["wd"], 16)
            sp.dma_start(wq, W_q.rearrange("(h p) d -> p h d", p=P)).then_inc(ld["wq"], 16)
            sp.dma_start(wuk[:, :, :], W_uk.rearrange("(h p) l -> p h l", p=P)).then_inc(ld["wuk"], 16)
            sp.dma_start(wo, W_o.rearrange("(c p) n -> p c n", p=P)).then_inc(ld["wo"], 16)
            sp.dma_start(wuv[:, :, :], W_uv.rearrange("(h p) l -> p h l", p=P)).then_inc(ld["wuv"], 16)

            sp.wait_ge(woT_ready, 8)
            with sp.Fori(0, NP // 2) as i:
                for r in range(2):
                    sp.wait_ge(u_hi, i * 4 + 2 * (r + 1))
                    sp.wait_ge(u_lo, i * 4 + 2 * (r + 1))
                    for side in range(2):
                        for part in range(2):
                            sp.dma_start(uc[LAT * part:LAT * (part + 1), bass.ds(i * 4 + 2 * r + side, 1), :],
                                         stage[LAT * side:LAT * (side + 1), r, part:part + 1, :]).then_inc(u_moved[r], 16)

            for n in range(NB):
                sp.wait_ge(x_added[2], n + 1)
                sp.dma_start(out_d[:, n, :], X[:, n, :]).then_inc(stored, 16)
            sp.wait_ge(stored, 16 * NB)

        @block.gpsimd
        def _(pool):
            nc.gpsimd.memset(ident[:, :], 0.0)
            nc.gpsimd.memset(tri[:, :], 1.0)
            nc.gpsimd.memset(onesb[:, :], 1.0)
            nc.gpsimd.memset(maskneg[:, :], 0.0)
            nc.gpsimd.memset(sel[:, :, :], 0.0)
            nc.gpsimd.memset(lat[:, :, LAT:LAT + 1], 1.0)
            nc.gpsimd.iota(rank_i[:, :, :], pattern=[[0, NB], [-1, E]], base=E, channel_multiplier=0).then_inc(const_step, 1)
            pool.wait_ge(const_step, 1)
            nc.gpsimd.affine_select(out=ident[:, :], in_=ident[:, :], compare_op=ALU.not_equal, fill=1.0,
                                    base=0, pattern=[[-1, P]], channel_multiplier=1)
            nc.gpsimd.affine_select(out=tri[:, :], in_=tri[:, :], compare_op=ALU.is_ge, fill=0.0,
                                    base=0, pattern=[[1, P]], channel_multiplier=-1)
            nc.gpsimd.affine_select(out=maskneg[:, :], in_=maskneg[:, :], compare_op=ALU.is_ge, fill=-1e30,
                                    base=0, pattern=[[-1, P]], channel_multiplier=1)
            nc.gpsimd.tensor_copy(rank[:, :, :], rank_i[:, :, :])
            nc.gpsimd.affine_select(out=sel[:, :, :], in_=sel[:, :, :], compare_op=ALU.not_equal, fill=1.0,
                                    base=0, pattern=[[EPC, FC], [1, EPC], [0, F]], channel_multiplier=-1).then_inc(const_step, 1)
            pool.wait_ge(const_step, 2)
            nc.gpsimd.tensor_copy(identb[:, :], ident[:, :])
            nc.gpsimd.affine_select(out=sel[:, :, :], in_=sel[:, :, :], compare_op=ALU.not_equal, fill=1.0,
                                    base=E, pattern=[[EPC, FC], [1, EPC], [0, F]], channel_multiplier=-1).then_inc(consts, 1)

            def ffn(L):
                k = 0
                for t in range(2):
                    for c in range(DC):
                        k += 1
                        pool.wait_ge(xThi_ready[2 * L], k)
                        nc.gpsimd.tensor_tensor(xT_lo[:, c, tokens(t)], xT[:, c, tokens(t)], xT_hi[:, c, tokens(t)],
                                                ALU.subtract).then_inc(xTlo_ready[2 * L], 1)
                k = 0
                for t in range(2):
                    for j in range(FC):
                        k += 1
                        pool.wait_ge(hThi_ready[L], k)
                        nc.gpsimd.tensor_tensor(hT_lo[:, j, tokens(t)], g[:, j, tokens(t)], hT_hi[:, j, tokens(t)],
                                                ALU.subtract).then_inc(hTlo_ready[L], 1)

            ffn(0)
            pool.wait_ge(n_hi, 4)
            with pool.Fori(0, H) as h:
                for b in range(B):
                    pool.wait_ge(ctx_free, h * B + (B + b + 1))
                    nc.gpsimd.tensor_copy(c_hi[:, SB * b:SB * (b + 1), bass.ts(h, LAT)], cst[:, b, :, :]).then_inc(chi_ready, 1)
                    pool.wait_ge(chi_ready, h * B + (b + 1))
                    nc.gpsimd.tensor_tensor(c_lo[:, SB * b:SB * (b + 1), bass.ts(h, LAT)], cst[:, b, :, :],
                                            c_hi[:, SB * b:SB * (b + 1), bass.ts(h, LAT)], ALU.subtract).then_inc(clo_ready, 1)
            ffn(1)

        @block.scalar
        def _(act):
            def layernorm_std(i):
                act.wait_ge(var_ready[i], 1)
                nc.scalar.activation(std[:, :], ve[:, :], ACT.Sqrt).then_inc(std_ready[i], 1)

            def ffn(L):
                for k in range(2 * DC):
                    t, c = divmod(k, DC)
                    act.wait_ge(xT_32[L], k + 1)
                    nc.scalar.copy(xT_hi[:, c, tokens(t)], xT[:, c, tokens(t)]).then_inc(xThi_ready[2 * L], 1)

                def copy_h1(s):
                    act.wait_ge(h_ps[L], s + 1)
                    if s >= 2:
                        act.wait_ge(z_ready[L], s - 1)
                    nc.scalar.copy(h1c[:, s % 2, :], bank[2 * (s % 2)][:, :]).then_inc(h1_ready[L], 1)

                def silu(s):
                    t, j = divmod(s, FC)
                    act.wait_ge(z_ready[L], s + 1)
                    nc.scalar.activation(g[:, j, tokens(t)], g[:, j, tokens(t)], ACT.Silu).then_inc(silu_ready[L], 1)

                act.wait_ge(dlt_ready[L], 1)
                nc.scalar.activation(e2[:, :], dlt[:, :], ACT.Exp).then_inc(e2_ready[L], 1)
                copy_h1(0)
                for s in range(1, 2 * FC):
                    copy_h1(s)
                    silu(s - 1)
                silu(2 * FC - 1)
                for s in range(2 * FC):
                    t, j = divmod(s, FC)
                    act.wait_ge(hw_ready[L], s + 1)
                    nc.scalar.copy(hT_hi[:, j, tokens(t)], g[:, j, tokens(t)]).then_inc(hThi_ready[L], 1)

            layernorm_std(0)
            for k, (src, dst) in enumerate(weight_splits()):
                act.wait_ge(w_ps, k + 1)
                nc.scalar.copy(dst[0], src).then_inc(w_hi, 1)
            ffn(0)

            for k in range(4):
                act.wait_ge(m_ps, k + 1)
                c, hg = divmod(k, 2)
                nc.scalar.activation(Mq[0][:, c, 8 * hg:8 * hg + 8, :].rearrange("p h l -> p (h l)"), bank[4 + k][:, :],
                                     ACT.Copy, scale=SCALE).then_inc(m_hi, 1)
            for k in range(8):
                act.wait_ge(woT_ps, k + 1)
                nc.scalar.copy(woT[:, 2 * k:2 * k + 2, :].rearrange("p h d -> p (h d)"), bank[k % 4][:, :]).then_inc(woT_ready, 1)
            layernorm_std(1)
            for k in range(4):
                act.wait_ge(n_ps, k + 1)
                nc.scalar.copy(Nv[0][:, 2 * k:2 * k + 2, :].rearrange("p h d -> p (h d)"), bank[4 + k][:, :]).then_inc(n_hi, 1)
            for k in range(2 * DC):
                t, c = divmod(k, DC)
                act.wait_ge(xT_ps[1], k + 1)
                nc.scalar.copy(xT_hi[:, c, tokens(t)], bank[k][:, :]).then_inc(xThi_ready[1], 1)
            for t in range(2):
                act.wait_ge(lat_ps, t + 1)
                nc.scalar.copy(latT_hi[:, tokens(t)], bank[4 + t][:, :]).then_inc(lat_hi, 1)
            act.wait_ge(lat_ps, 3)
            nc.scalar.copy(lat[:, :, 0:LAT], bank[6][:, :].rearrange("p (n l) -> p n l", n=NB)).then_inc(lat_hi, 1)

            with act.Fori(0, NP // 2) as i:
                for r in range(2):
                    act.wait_ge(u_moved[r], i * 64)
                    for t in range(2):
                        act.wait_ge(u_ps, i * 4 + (2 * r + t + 1))
                        nc.scalar.copy(stage[:, r, 0, tokens(t)], bank[2 * r + t][:, :]).then_inc(u_hi, 1)

            def split(u, waited):
                n = P * (u % SB + 1)
                act.wait_ge(pT_ps, waited)
                nc.scalar.copy(pT_hi[:, u % 2, 0:n], bank[4 + u % 2][:, 0:n]).then_inc(pThi_ready, 1)

            def exponent(u, waited):
                n = P * (u % SB + 1)
                act.wait_ge(max_ready, waited)
                nc.scalar.activation(prob[:, u % 4, 0:n], bank[u % 4][:, 0:n], ACT.Exp,
                                     bias=nmax[:, u:u + 1]).then_inc(prob_ready, 1)

            for u in range(4):
                exponent(u, u + 1)
            for u in range(2):
                split(u, u + 1)
            with act.Fori(0, H - 1) as h:
                for j in range(UNITS):
                    split((j + 2) % UNITS, h * UNITS + (j + 3))
                    exponent((j + 4) % UNITS, h * UNITS + (j + 5))
            for j in range(UNITS):
                if j + 2 < UNITS:
                    split(j + 2, (H - 1) * UNITS + j + 3)
                if j + 4 < UNITS:
                    exponent(j + 4, (H - 1) * UNITS + j + 5)

            with act.Fori(0, NB // 2) as i:
                for r in range(2):
                    act.wait_ge(cT_ps, i * 2 + (r + 1))
                    nc.scalar.copy(stage[:, r, 0, :], bank[2 * r][:, :].bitcast(BF16)).then_inc(cThi_ready, 1)

            layernorm_std(2)
            ffn(1)

        @block.vector
        def _(dve):
            steps = [0]

            def link(ins):
                steps[0] += 1
                ins.then_inc(dve_step, 1)
                dve.wait_ge(dve_step, steps[0])

            def layernorm(i):
                for n in range(NB):
                    if i == 0 and n % HB == 0:
                        dve.wait_ge(ld["x0"] if n == 0 else ld["x1"], 16)
                    last = nc.vector.bn_stats(st[:, n, :], X[:, n, :])
                link(last)
                for n in range(NB):
                    last = nc.vector.bn_aggr(mv[:, n, :], st[:, n, :])
                link(last)
                nc.vector.tensor_scalar_add(ve[:, :], mv[:, :, 1], EPS).then_inc(var_ready[i], 1)
                dve.wait_ge(std_ready[i], 1)
                link(nc.vector.reciprocal(rstd[:, :], std[:, :]))
                for n in range(NB):
                    nc.vector.tensor_scalar(xn[:, n, :], X[:, n, :], mv[:, n, 0:1], rstd[:, n:n + 1],
                                            ALU.subtract, ALU.mult).then_inc(xn_ready[i], 1)

            def over_experts(v):
                return v.unsqueeze(2).to_broadcast([P, NB, E])

            def choose(src, k):
                link(nc.vector.reduce_max(top[:, k, :], src, AX.X))
                link(nc.vector.tensor_tensor(eq[:, :, :], src, over_experts(top[:, k, :]), ALU.is_equal))
                link(nc.vector.tensor_tensor(tb[:, :, :], eq[:, :, :], rank[:, :, :], ALU.mult))
                link(nc.vector.reduce_max(tr[:, k, :], tb[:, :, :], AX.X))
                link(nc.vector.tensor_tensor(chosen[:, k, :, :], tb[:, :, :], over_experts(tr[:, k, :]), ALU.is_equal))

            def ffn(L):
                for k in range(2 * DC):
                    t, c = divmod(k, DC)
                    dve.wait_ge(xT_ps[2 * L], k + 1)
                    nc.vector.tensor_copy(xT[:, c, tokens(t)], bank[k][:, :]).then_inc(xT_32[L], 1)

                dve.wait_ge(lg_ps[L], 1)
                link(nc.vector.tensor_copy(lg[:, :, :], bank[4][:, 0:NB * E].rearrange("p (n e) -> p n e", n=NB)))
                choose(lg[:, :, :], 0)
                link(nc.vector.tensor_scalar(cp[:, :, :], chosen[:, 0, :, :], -0.5, -2.0 * HUGE / 2.0, ALU.add, ALU.mult))
                link(nc.vector.tensor_tensor(l2[:, :, :], lg[:, :, :], cp[:, :, :], ALU.min))
                choose(l2[:, :, :], 1)
                nc.vector.tensor_tensor(dlt[:, :], top[:, 1, :], top[:, 0, :], ALU.subtract).then_inc(dlt_ready[L], 1)
                dve.wait_ge(dlt_ready[L], 1)

                def product(s):
                    t, j = divmod(s, FC)
                    dve.wait_ge(h1_ready[L], s + 1)
                    nc.vector.tensor_tensor(g[:, j, tokens(t)], h1c[:, s % 2, :], bank[2 * (s % 2) + 1][:, :],
                                            ALU.mult).then_inc(z_ready[L], 1)

                product(0)
                product(1)

                dve.wait_ge(e2_ready[L], 1)
                link(nc.vector.tensor_scalar_add(den[:, :], e2[:, :], 1.0))
                link(nc.vector.reciprocal(rec[:, :], den[:, :]))
                nc.vector.tensor_scalar(rw[:, 0, :], rec[:, :], 0.5, None, ALU.mult)
                link(nc.vector.scalar_tensor_tensor(out=rw[:, 1, :], in0=rec[:, :], scalar=0.5, in1=e2[:, :],
                                                    op0=ALU.mult, op1=ALU.mult))
                dve.wait_ge(pos_ps[L], 1)
                link(nc.vector.scalar_tensor_tensor(
                    out=kept[:, :, :, :].rearrange("p s n e -> p (s n e)"), in0=bank[5][:, 0:2 * NB * E],
                    scalar=float(CAP), in1=chosen[:, :, :, :].rearrange("p s n e -> p (s n e)"),
                    op0=ALU.is_le, op1=ALU.mult))
                for k in range(2):
                    last = nc.vector.tensor_tensor(kept[:, k, :, :], kept[:, k, :, :], over_experts(rw[:, k, :]), ALU.mult)
                link(last)
                link(nc.vector.tensor_tensor(wgt[:, :, :], kept[:, 0, :, :], kept[:, 1, :, :], ALU.add))
                link(nc.vector.tensor_copy(wgt_hl[:, :, 0, :], wgt[:, :, :]))
                nc.vector.tensor_tensor(wgt_hl[:, :, 1, :], wgt[:, :, :], wgt_hl[:, :, 0, :],
                                        ALU.subtract).then_inc(wgt_ready[L], 1)
                product(2)
                product(3)
                dve.wait_ge(wgtT_ps[L], 1)
                nc.vector.tensor_copy(wgtT[:, :], bank[6][0:2 * E, :].bitcast(BF16)).then_inc(wgtT_ready[L], 1)
                product(4)
                product(5)
                for s in range(2 * FC):
                    t, j = divmod(s, FC)
                    dve.wait_ge(wexp_ps[L], s + 1)
                    dve.wait_ge(silu_ready[L], s + 1)
                    nc.vector.tensor_tensor(g[:, j, tokens(t)], g[:, j, tokens(t)], bank[5 + 2 * (s % 2)][:, :],
                                            ALU.mult).then_inc(hw_ready[L], 1)
                for n in range(NB):
                    dve.wait_ge(y_ps[L], n + 1)
                    nc.vector.tensor_tensor(X[:, n, :], X[:, n, :], bank[n % 4][:, 0:D], ALU.add).then_inc(x_added[2 * L], 1)
                dve.wait_ge(x_added[2 * L], NB)

            layernorm(0)
            for k, (src, dst) in enumerate(weight_splits()):
                dve.wait_ge(w_hi, k + 1)
                nc.vector.tensor_tensor(dst[1], src, dst[0], ALU.subtract).then_inc(w_lo, 1)
            nc.vector.tensor_copy(gateT[:, :, :], bank[6][:, 0:DC * E].rearrange("p (c e) -> p c e", c=DC)).then_inc(w_lo, 1)
            dve.wait_ge(consts, 1)
            ffn(0)

            layernorm(1)
            for k in range(4):
                dve.wait_ge(m_hi, k + 1)
                c, hg = divmod(k, 2)
                hi, lo = (m[:, c, 8 * hg:8 * hg + 8, :].rearrange("p h l -> p (h l)") for m in Mq)
                nc.vector.scalar_tensor_tensor(out=lo, in0=bank[4 + k][:, :], scalar=SCALE, in1=hi,
                                               op0=ALU.mult, op1=ALU.subtract).then_inc(m_lo, 1)
            for k in range(4):
                dve.wait_ge(n_hi, k + 1)
                hi, lo = (m[:, 2 * k:2 * k + 2, :].rearrange("p h d -> p (h d)") for m in Nv)
                nc.vector.tensor_tensor(lo, bank[4 + k][:, :], hi, ALU.subtract).then_inc(n_lo, 1)
            for k in range(2 * DC):
                t, c = divmod(k, DC)
                dve.wait_ge(xThi_ready[1], k + 1)
                nc.vector.tensor_tensor(xT_lo[:, c, tokens(t)], bank[k][:, :], xT_hi[:, c, tokens(t)],
                                        ALU.subtract).then_inc(xTlo_ready[1], 1)
            for t in range(2):
                dve.wait_ge(lat_hi, t + 1)
                nc.vector.tensor_tensor(latT_lo[:, tokens(t)], bank[4 + t][:, :], latT_hi[:, tokens(t)],
                                        ALU.subtract).then_inc(lat_lo, 1)
            dve.wait_ge(lat_hi, 3)
            nc.vector.tensor_tensor(lat[:, :, LAT + 1:2 * LAT + 1], bank[6][:, :].rearrange("p (n l) -> p n l", n=NB),
                                    lat[:, :, 0:LAT], ALU.subtract).then_inc(lat_lo, 1)

            with dve.Fori(0, NP // 2) as i:
                for r in range(2):
                    for t in range(2):
                        dve.wait_ge(u_hi, i * 4 + (2 * r + t + 1))
                        nc.vector.tensor_tensor(stage[:, r, 1, tokens(t)], bank[2 * r + t][:, :], stage[:, r, 0, tokens(t)],
                                                ALU.subtract).then_inc(u_lo, 1)

            nc.vector.memset(rsum[:, :, :], 0.0).then_inc(ctx_free, B)

            def row_max(u, waited):
                n = P * (u % SB + 1)
                dve.wait_ge(s_ps, waited)
                nc.vector.tensor_reduce(nmax[:, u:u + 1], bank[u % 4][:, 0:n], AX.X, ALU.max, negate=True).then_inc(max_ready, 1)

            def split(u, waited):
                n = P * (u % SB + 1)
                dve.wait_ge(pThi_ready, waited)
                nc.vector.tensor_tensor(pT_lo[:, u % 2, 0:n], bank[4 + u % 2][:, 0:n], pT_hi[:, u % 2, 0:n],
                                        ALU.subtract).then_inc(pTlo_ready, 1)

            def normalise(b, waited, done):
                src = bank[6 + b][:, 0:SB * (LAT + 1)].rearrange("p (q l) -> p q l", q=SB)
                dve.wait_ge(ctx_ps, waited)
                nc.vector.reciprocal(rsum[:, b, :], src[:, :, LAT]).then_inc(rsum_ready, 1)
                dve.wait_ge(rsum_ready, done)
                nc.vector.tensor_tensor(cst[:, b, :, :], src[:, :, 0:LAT],
                                        rsum[:, b, :].unsqueeze(2).to_broadcast([P, SB, LAT]), ALU.mult).then_inc(ctx_free, 1)

            for u in range(4):
                row_max(u, u + 1)
            for u in range(2):
                split(u, u + 1)
            with dve.Fori(0, H - 1) as h:
                for j in range(UNITS):
                    split((j + 2) % UNITS, h * UNITS + (j + 3))
                    row_max((j + 4) % UNITS, h * UNITS + (j + 5))
                    if j % SB == SB - 1:
                        dve.wait_ge(clo_ready, h * B)
                        normalise(j // SB, h * B + (j // SB + 1), h * B + (j // SB + 1))
            for j in range(UNITS):
                if j + 2 < UNITS:
                    split(j + 2, (H - 1) * UNITS + j + 3)
                if j + 4 < UNITS:
                    row_max(j + 4, (H - 1) * UNITS + j + 5)
                if j % SB == SB - 1:
                    dve.wait_ge(clo_ready, (H - 1) * B)
                    normalise(j // SB, (H - 1) * B + j // SB + 1, (H - 1) * B + j // SB + 1)

            def context_lo(r, waited):
                dve.wait_ge(cThi_ready, waited)
                nc.vector.tensor_copy(stage[:, r, 1, :], bank[2 * r + 1][:, :].bitcast(BF16)).then_inc(cTlo_ready, 1)

            def add_attention(r, n, waited):
                dve.wait_ge(attn_ps, waited)
                nc.vector.tensor_tensor(X[:, bass.ds(n, 1), :], X[:, bass.ds(n, 1), :],
                                        bank[4 + r][:, 0:D].unsqueeze(1), ALU.add).then_inc(x_added[1], 1)

            context_lo(0, 1)
            with dve.Fori(0, NB // 2 - 1) as i:
                context_lo(1, i * 2 + 2)
                add_attention(0, i * 2, i * 2 + 1)
                context_lo(0, i * 2 + 3)
                add_attention(1, i * 2 + 1, i * 2 + 2)
            context_lo(1, NB)
            add_attention(0, NB - 2, NB - 1)
            add_attention(1, NB - 1, NB)
            dve.wait_ge(x_added[1], NB)

            layernorm(2)
            ffn(1)

        @block.tensor
        def _(pe):
            mm = nc.tensor.matmul

            def split_product(dst, left, right, K, start=True, stop=True):
                terms = [(0, 0, k) for k in range(K)] + [(0, 1, k) for k in range(K)] + [(1, 0, k) for k in range(K)]
                for n, (a, b, k) in enumerate(terms):
                    last = mm(dst, left(k)[a], right(k)[b], start=start and n == 0, stop=stop and n == len(terms) - 1)
                return last

            def transpose_xn(i):
                for t in range(2):
                    pe.wait_ge(xn_ready[i], HB * (t + 1))
                    for c in range(DC):
                        for n in range(HB):
                            last = nc.tensor.transpose(bank[DC * t + c][:, blk(n)], xn[:, HB * t + n, blk(c)], ident[:, :])
                        last.then_inc(xT_ps[i], 1)

            def ffn(L):
                transpose_xn(2 * L)
                pe.wait_ge(xT_32[L], 2 * DC)
                for n in range(NB):
                    for c in range(DC):
                        last = mm(bank[4][:, n * E:(n + 1) * E], xT[:, c, blk(n)], gateT[:, c, :], start=(c == 0), stop=(c == DC - 1))
                last.then_inc(lg_ps[L], 1)

                def hidden(s):
                    t, j = divmod(s, FC)
                    if j == 0:
                        pe.wait_ge(xTlo_ready[2 * L], DC * (t + 1))
                    if s >= 2:
                        pe.wait_ge(z_ready[L], s - 1)
                    for n, wT in enumerate((w1T, w3T)):
                        last = split_product(bank[2 * (s % 2) + n][:, :],
                                             lambda k: [w[:, k, blk(j)] for w in wT],
                                             lambda k: [xT_hi[:, k, tokens(t)], xT_lo[:, k, tokens(t)]], DC)
                    last.then_inc(h_ps[L], 1)

                hidden(0)
                hidden(1)
                pe.wait_ge(dlt_ready[L], 1)
                picks = chosen[:, :, :, :].rearrange("p s n e -> p (s n e)")
                G = 2 * NB
                mm(bank[5][:, 0:G * E], tri[:, :], picks, start=True, stop=False)
                for k in range(1, G):
                    last = mm(bank[5][:, k * E:G * E], onesb[:, :], picks[:, 0:(G - k) * E], start=False, stop=(k == G - 1))
                last.then_inc(pos_ps[L], 1)
                hidden(2)
                hidden(3)
                pe.wait_ge(wgt_ready[L], 1)
                for n in range(NB):
                    last = nc.tensor.transpose(bank[6][0:2 * E, :].bitcast(BF16)[:, blk(n)],
                                               wgt_hl[:, n, :, :].rearrange("p a e -> p (a e)"), identb[:, :])
                last.then_inc(wgtT_ps[L], 1)
                hidden(4)
                hidden(5)
                pe.wait_ge(wgtT_ready[L], 1)
                for s in range(2 * FC):
                    t, j = divmod(s, FC)
                    if s >= 2:
                        pe.wait_ge(hw_ready[L], s - 1)
                    mm(bank[5 + 2 * (s % 2)][:, :], sel[:, j, :], wgtT[:, tokens(t)], start=True, stop=True).then_inc(wexp_ps[L], 1)
                pe.wait_ge(z_ready[L], 2 * FC)
                for n in range(NB):
                    pe.wait_ge(hTlo_ready[L], FC * (n // HB + 1))
                    if n >= 4:
                        pe.wait_ge(x_added[2 * L], n - 3)
                    split_product(bank[n % 4][:, 0:D], lambda k: [hT_hi[:, k, blk(n)], hT_lo[:, k, blk(n)]],
                                  lambda k: [w[:, k, :] for w in w2T], FC).then_inc(y_ps[L], 1)

            pe.wait_ge(consts, 1)
            for n, (wn, key) in enumerate(((w1n, "w1"), (w3n, "w3"))):
                pe.wait_ge(ld[key], 16)
                for c in range(DC):
                    for j in range(FC):
                        last = nc.tensor.transpose(bank[2 * n + c][:, blk(j)], wn[:, j, blk(c)], ident[:, :])
                    last.then_inc(w_ps, 1)
            pe.wait_ge(ld["w2"], 16 * DC)
            for j in range(FC):
                for c in range(DC):
                    at = (j % 2) * D + c * P
                    last = nc.tensor.transpose(bank[4 + j // 2][:, at:at + P], w2n[:, c, blk(j)], ident[:, :])
                if j >= 1:
                    last.then_inc(w_ps, 1)
            pe.wait_ge(ld["gate"], 16)
            pe.wait_ge(ld["wd"], 16)
            for c in range(DC):
                nc.tensor.transpose(bank[6][:, c * E:(c + 1) * E], gaten[:, blk(c)], ident[0:E, 0:E])
            for c in range(DC):
                last = nc.tensor.transpose(bank[6][:, P + c * LAT:P + (c + 1) * LAT], wdn[:, blk(c)], ident[0:LAT, 0:LAT])
            last.then_inc(w_ps, 1)
            pe.wait_ge(w_lo, N_W + 1)
            ffn(0)

            pe.wait_ge(ld["wq"], 16)
            pe.wait_ge(ld["wuk"], 16)
            for k in range(4):
                c, hg = divmod(k, 2)
                for h in range(8):
                    last = mm(bank[4 + k][:, LAT * h:LAT * (h + 1)], wq[:, 8 * hg + h, blk(c)], wuk[:, 8 * hg + h, :], start=True, stop=True)
                last.then_inc(m_ps, 1)
            pe.wait_ge(x_added[0], NB)
            pe.wait_ge(ld["wo"], 16)
            for k in range(8):
                if k >= 4:
                    pe.wait_ge(woT_ready, k - 3)
                for h in range(2):
                    for c in range(DC):
                        at = D * h + P * c
                        last = nc.tensor.transpose(bank[k % 4][:, at:at + P], wo[:, c, blk(2 * k + h)], ident[:, :])
                last.then_inc(woT_ps, 1)
            pe.wait_ge(ld["wuv"], 16)
            for k in range(4):
                pe.wait_ge(m_lo, k + 1)
                pe.wait_ge(woT_ready, 2 * k + 2)
                for h in range(4):
                    side = h % 2
                    last = mm(bank[4 + k][LAT * side:LAT * (side + 1), D * (h // 2):D * (h // 2 + 1)],
                              wuv[:, 4 * k + h, :], woT[:, 4 * k + h, :], start=True, stop=True)
                last.then_inc(n_ps, 1)

            pe.wait_ge(woT_ready, 8)
            transpose_xn(1)
            for t in range(2):
                pe.wait_ge(n_lo, t + 1)
                pe.wait_ge(xTlo_ready[1], DC * (t + 1))
                split_product(bank[4 + t][:, :],
                              lambda k: [w[:, k, :, :].rearrange("p r l -> p (r l)") for w in wdT],
                              lambda k: [xT_hi[:, k, tokens(t)], xT_lo[:, k, tokens(t)]], DC).then_inc(lat_ps, 1)
            pe.wait_ge(n_lo, 3)
            for n in range(NB):
                last = split_product(bank[6][:, LAT * n:LAT * (n + 1)],
                                     lambda k: [xT_hi[:, k, blk(n)], xT_lo[:, k, blk(n)]],
                                     lambda k: [w[:, k, 0, :] for w in wdT], DC)
            last.then_inc(lat_ps, 1)

            def queries(i, r, reuse):
                for t in range(2):
                    if reuse is not None:
                        pe.wait_ge(u_lo, reuse + t)
                    last = split_product(bank[2 * r + t][:, :],
                                         lambda k: [m[:, k, bass.ds(i * 4 + 2 * r, 2), :].rearrange("p h l -> p (h l)") for m in Mq],
                                         lambda k: [xT_hi[:, k, tokens(t)], xT_lo[:, k, tokens(t)]], DC)
                    last.then_inc(u_ps, 1)

            for r in range(2):
                queries(0, r, None)
            with pe.Fori(1, NP // 2) as i:
                for r in range(2):
                    queries(i, r, i * 4 + (2 * r + 1 - 4))

            pe.wait_ge(lat_lo, 3)
            pe.wait_ge(n_lo, 4)
            pe.wait_ge(u_lo, 2 * NP)
            for r in range(2):
                pe.wait_ge(u_moved[r], 64 * (NP // 2))

            def scores(u, h):
                b, q = divmod(u, SB)
                n = P * (q + 1)
                dst = bank[u % 4]
                keys = slice(SEQ * b, SEQ * b + n)
                at = SEQ * b + P * q
                mm(dst[:, 0:n], uc[:, h, at:at + P], latT_hi[:, keys], start=True, stop=False)
                mm(dst[:, 0:n], uc[0:LAT, h, at:at + P], latT_lo[0:LAT, keys], start=False, stop=False)
                mm(dst[:, n - P:n], identb[:, :], maskneg[:, :], start=False, stop=True).then_inc(s_ps, 1)

            def transposes(u, waited):
                pe.wait_ge(prob_ready, waited)
                for k in range(u % SB + 1):
                    last = nc.tensor.transpose(bank[4 + u % 2][:, blk(k)], prob[:, u % 4, blk(k)], ident[:, :])
                last.then_inc(pT_ps, 1)

            def context(u, waited, free):
                b, q = divmod(u, SB)
                if q == 0:
                    pe.wait_ge(ctx_free, free)
                pe.wait_ge(pTlo_ready, waited)
                dst = bank[6 + b]
                at = q * (LAT + 1)
                for k in range(q + 1):
                    n = SB * b + k
                    mm(dst[:, at:at + LAT + 1], pT_hi[:, u % 2, blk(k)], lat[:, n, 0:LAT + 1], start=(k == 0), stop=False)
                    mm(dst[:, at:at + LAT], pT_hi[:, u % 2, blk(k)], lat[:, n, LAT + 1:2 * LAT + 1], start=False, stop=False)
                    last = mm(dst[:, at:at + LAT + 1], pT_lo[:, u % 2, blk(k)], lat[:, n, 0:LAT + 1], start=False, stop=(k == q))
                if q == SB - 1:
                    last.then_inc(ctx_ps, 1)

            for u in range(4):
                scores(u, 0)
            for u in range(2):
                transposes(u, u + 1)
            with pe.Fori(0, H - 1) as h:
                for j in range(UNITS):
                    context(j, h * UNITS + (j + 1), h * B + (j // SB + 1))
                    transposes((j + 2) % UNITS, h * UNITS + (j + 3))
                    scores((j + 4) % UNITS, h + (j + 4) // UNITS)
            for j in range(UNITS):
                context(j, (H - 1) * UNITS + j + 1, (H - 1) * B + j // SB + 1)
                if j + 2 < UNITS:
                    transposes(j + 2, (H - 1) * UNITS + j + 3)
                if j + 4 < UNITS:
                    scores(j + 4, H - 1)

            pe.wait_ge(clo_ready, B * H)

            def transpose_context(r, n):
                for part, src in enumerate((c_hi, c_lo)):
                    for k in range(NP):
                        last = nc.tensor.transpose(bank[2 * r + part][:, :].bitcast(BF16)[:, blk(k)], src[:, n, blk(k)], identb[:, :])
                last.then_inc(cT_ps, 1)

            def project(r, waited):
                pe.wait_ge(cTlo_ready, waited)
                split_product(bank[4 + r][:, 0:D],
                              lambda k: [stage[:, r, part, blk(k)] for part in range(2)],
                              lambda k: [m[:, k, :] for m in Nv], NP).then_inc(attn_ps, 1)

            transpose_context(0, 0)
            with pe.Fori(0, NB // 2 - 1) as i:
                transpose_context(1, i * 2 + 1)
                project(0, i * 2 + 1)
                transpose_context(0, i * 2 + 2)
                project(1, i * 2 + 2)
            transpose_context(1, NB - 1)
            project(0, NB - 1)
            project(1, NB)

            ffn(1)


_INS = ['L0_attn_x', 'L0_attn_W_down', 'L0_attn_W_uk', 'L0_attn_W_uv', 'L0_attn_W_q', 'L0_attn_W_o',
        'L0_ffn_gate_w', 'L0_ffn_w1', 'L0_ffn_w2', 'L0_ffn_w3']
_OUTS = [((2, 512, 256), 'float32')]


def kernel(**inputs):
    import numpy as _np
    import concourse.bacc as _bacc
    from concourse import mybir as _mybir
    from concourse.bass_utils import run_bass_kernel_spmd as _run

    nc = _bacc.Bacc("TRN2", target_bir_lowering=False, num_devices=1)
    arrays, args = {}, []
    for name in _INS:
        a = _np.ascontiguousarray(inputs[name])
        arrays[f"in_{name}_dram"] = a
        args.append(nc.dram_tensor(f"in_{name}_dram", a.shape, _mybir.dt.from_np(a.dtype), kind="ExternalInput").ap())
    for i, (shape, dtype) in enumerate(_OUTS):
        dt = _mybir.dt.from_np(_np.dtype(dtype))
        args.append(nc.dram_tensor(f"out_{i}_dram", shape, dt, kind="ExternalOutput").ap())
    bass_macaron_moe_mla_moe(nc, *args)
    r = _run(nc, [arrays], core_ids=[0])
    got = tuple(r.results[0][f"out_{i}_dram"] for i in range(len(_OUTS)))
    return got[0]
```

```python
import concourse.bass as bass
from concourse import mybir
from contextlib import ExitStack


def bass_macaron_moe_mla_moe(
    nc: bass.Bass,
    x_in: bass.AP,
    W_down: bass.AP,
    W_uk: bass.AP,
    W_uv: bass.AP,
    W_q: bass.AP,
    W_o: bass.AP,
    gate_w: bass.AP,
    w1: bass.AP,
    w2: bass.AP,
    w3: bass.AP,
    out: bass.AP,
):
    F32 = mybir.dt.float32
    BF16 = mybir.dt.bfloat16
    FP16 = mybir.dt.float16
    I32 = mybir.dt.int32
    ALU = mybir.AluOpType
    ACT = mybir.ActivationFunctionType
    AX = mybir.AxisListType

    P = 128
    B, SEQ, D = x_in.shape
    T = B * SEQ
    NB = T // P
    SB = SEQ // P
    DC = D // P
    HALF = T // 2
    HB = HALF // P
    E, F, _ = w1.shape
    EF = E * F
    FC = EF // P
    EPC = P // F
    CAP = -(-T * 5 // (E * 4))
    LAT = W_down.shape[0]
    H = W_uk.shape[0] // P
    NP = H // 2
    SCALE = 1.0 / float(P) ** 0.5
    EPS = 1e-5
    HUGE = 1.5e38
    HEAD_UNITS = [[(0, 2, 0), (0, 0, 3 * P)], [(0, 3, 0)], [(0, 1, 0), (1, 1, 2 * P)],
                  [(1, 2, 0), (1, 0, 3 * P)], [(1, 3, 0)]]
    HU = len(HEAD_UNITS)
    UNITS = 2 * HU
    SEQ_DONE = {2: 0, 4: 1}
    SCORE_BANK = [0, 1, 2, 0, 1, 2, 0, 1, 2, 1]
    HELD_BY = [-4, -1, -2, 0, 1, 2, 3, 4, 5, 7]

    x_d = x_in.rearrange("b s d -> (b s) d").rearrange("(n p) d -> p n d", p=P)
    out_d = out.rearrange("b s d -> (b s) d").rearrange("(n p) d -> p n d", p=P)

    ctx = ExitStack()
    with ctx:
        def sb(name, shape, dt):
            return ctx.enter_context(nc.sbuf_tensor(name, shape, dt))

        def sem(name):
            return ctx.enter_context(nc.semaphore(name))

        ident = sb("ident", [P, P], F32)
        identb = sb("identb", [P, P], BF16)
        tri = sb("tri", [P, P], BF16)
        onesb = sb("onesb", [P, P], BF16)
        maskneg = sb("maskneg", [P, P], BF16)
        rank_i = sb("rank_i", [P, NB, E], I32)
        rank = sb("rank", [P, NB, E], F32)
        sel = sb("sel", [2 * E, FC, P], BF16)

        X = sb("X", [P, NB, D], F32)
        xn = sb("xn", [P, NB, D], F32)
        xT = sb("xT", [P, DC, T], F32)
        xT_hi = sb("xT_hi", [P, DC, T], FP16)
        xT_lo = sb("xT_lo", [P, DC, T], FP16)
        st = sb("st", [P, NB, 6], F32)
        mv = sb("mv", [P, NB, 2], F32)
        ve = sb("ve", [P, NB], F32)
        std = sb("std", [P, NB], F32)
        rstd = sb("rstd", [P, NB], F32)

        ffn_buf = sb("ffn_buf", [P, 4, T], F32)
        g = ffn_buf[:, 0:FC, :]
        h1c = ffn_buf[:, FC, :].rearrange("p (b n) -> p b n", b=2)
        hT_hi = sb("hT_hi", [P, FC, T], BF16)
        hT_lo = sb("hT_lo", [P, FC, T], BF16)
        lg = sb("lg", [P, NB, E], F32)
        eq = sb("eq", [P, NB, E], F32)
        tb = sb("tb", [P, NB, E], F32)
        cp = sb("cp", [P, NB, E], F32)
        l2 = sb("l2", [P, NB, E], F32)
        top = sb("top", [P, 2, NB], F32)
        tr = sb("tr", [P, 2, NB], F32)
        dlt = sb("dlt", [P, NB], F32)
        e2 = sb("e2", [P, NB], F32)
        den = sb("den", [P, NB], F32)
        rec = sb("rec", [P, NB], F32)
        rw = sb("rw", [P, 2, NB], F32)
        chosen = sb("chosen", [P, 2, NB, E], BF16)
        kept = sb("kept", [P, 2, NB, E], F32)
        wgt = sb("wgt", [P, NB, E], F32)
        wgt_hl = sb("wgt_hl", [P, NB, 2, E], BF16)
        wgtT = sb("wgtT", [2 * E, T], BF16)

        w1n = sb("w1n", [P, FC, D], F32)
        w3n = sb("w3n", [P, FC, D], F32)
        w2n = sb("w2n", [P, DC, EF], F32)
        gaten = sb("gaten", [E, D], F32)
        wdn = sb("wdn", [LAT, D], F32)
        gateT = sb("gateT", [P, DC, E], F32)
        w1T = [sb("w1T_hi", [P, DC, EF], BF16), sb("w1T_lo", [P, DC, EF], BF16)]
        w3T = [sb("w3T_hi", [P, DC, EF], BF16), sb("w3T_lo", [P, DC, EF], BF16)]
        w2T = [sb("w2T_hi", [P, FC, D], BF16), sb("w2T_lo", [P, FC, D], BF16)]
        wdT = [sb("wdT_hi", [P, DC, 2, LAT], BF16), sb("wdT_lo", [P, DC, 2, LAT], BF16)]
        wuk = sb("wuk", [P, H, LAT], F32)
        wuv = sb("wuv", [P, H, LAT], F32)
        wqo = sb("wqo", [P, 2, H * D], F32)
        wq = wqo[:, 0, :].rearrange("p (h d) -> p h d", h=H)
        wo = wqo[:, 1, :].rearrange("p (c n) -> p c n", c=DC)
        uc = wqo[:, :, :].rearrange("p a n -> p (a n)").bitcast(BF16).rearrange("p (h t) -> p h t", h=H)
        woT_buf = sb("woT_buf", [P, H * D], F32)
        woT = woT_buf[:, :].rearrange("p (h d) -> p h d", h=H)
        c_hi = woT_buf[:, :].bitcast(BF16).rearrange("p (n c) -> p n c", n=NB)
        c_lo = ffn_buf[:, :, :].rearrange("p a n -> p (a n)").bitcast(BF16).rearrange("p (n c) -> p n c", n=NB)
        Mq = [sb("Mq_hi", [P, DC, H, LAT], BF16), sb("Mq_lo", [P, DC, H, LAT], BF16)]
        Nv = [sb("Nv_hi", [P, NP, D], BF16), sb("Nv_lo", [P, NP, D], BF16)]

        latT_hi = sb("latT_hi", [P, T], BF16)
        latT_lo = sb("latT_lo", [P, T], BF16)
        lat = sb("lat", [P, NB, 2 * LAT + 1], BF16)
        stage = sb("stage", [P, 2, 2, T], BF16)
        prob = sb("prob", [P, 2, SEQ], F32)
        pT_hi = sb("pT_hi", [P, 2, SEQ], FP16)
        pT_lo = sb("pT_lo", [P, 2, SEQ], FP16)
        nmax = sb("nmax", [P, UNITS, 2], F32)
        rsum = sb("rsum", [P, B, SB], F32)
        cst = sb("cst", [P, B, SB, LAT], F32)

        bank = [ctx.enter_context(nc.psum_tensor(f"bank{i}", [P, 512], F32)) for i in range(8)]

        ld = {n: sem(f"ld_{n}") for n in ("x0", "x1", "gate", "w1", "w3", "w2", "wd", "wq", "wuk", "wuv", "wo")}
        consts = sem("consts")
        const_step = sem("const_step")
        var_ready = [sem(f"var_ready{i}") for i in range(3)]
        std_ready = [sem(f"std_ready{i}") for i in range(3)]
        xn_ready = [sem(f"xn_ready{i}") for i in range(3)]
        xT_ps = [sem(f"xT_ps{i}") for i in range(3)]
        xT_32 = [sem(f"xT_32_{i}") for i in range(2)]
        xThi_ready = [sem(f"xThi_ready{i}") for i in range(3)]
        xTlo_ready = [sem(f"xTlo_ready{i}") for i in range(3)]
        lg_ps = [sem(f"lg_ps{i}") for i in range(2)]
        dlt_ready = [sem(f"dlt_ready{i}") for i in range(2)]
        e2_ready = [sem(f"e2_ready{i}") for i in range(2)]
        pos_ps = [sem(f"pos_ps{i}") for i in range(2)]
        wgt_ready = [sem(f"wgt_ready{i}") for i in range(2)]
        wgtT_ps = [sem(f"wgtT_ps{i}") for i in range(2)]
        wgtT_ready = [sem(f"wgtT_ready{i}") for i in range(2)]
        h_ps = [sem(f"h_ps{i}") for i in range(2)]
        h1_ready = [sem(f"h1_ready{i}") for i in range(2)]
        z_ready = [sem(f"z_ready{i}") for i in range(2)]
        silu_ready = [sem(f"silu_ready{i}") for i in range(2)]
        wexp_ps = [sem(f"wexp_ps{i}") for i in range(2)]
        hw_ready = [sem(f"hw_ready{i}") for i in range(2)]
        hThi_ready = [sem(f"hThi_ready{i}") for i in range(2)]
        hTlo_pool = [sem(f"hTlo_pool{i}") for i in range(2)]
        hTlo_dve = [sem(f"hTlo_dve{i}") for i in range(2)]
        y_ps = [sem(f"y_ps{i}") for i in range(2)]
        x_added = [sem(f"x_added{i}") for i in range(3)]
        w_ps = sem("w_ps")
        w_hi = sem("w_hi")
        w_lo = sem("w_lo")
        m_ps = sem("m_ps")
        m_hi = sem("m_hi")
        m_lo = sem("m_lo")
        woT_ps = sem("woT_ps")
        woT_ready = sem("woT_ready")
        n_ps = sem("n_ps")
        n_hi = sem("n_hi")
        n_lo = sem("n_lo")
        lat_ps = sem("lat_ps")
        lat_hi = sem("lat_hi")
        lat_lo = sem("lat_lo")
        u_ps = sem("u_ps")
        u_hi = sem("u_hi")
        u_lo = sem("u_lo")
        u_moved = sem("u_moved")
        s_ps = sem("s_ps")
        max_ready = sem("max_ready")
        prob_ready = sem("prob_ready")
        pT_ps = sem("pT_ps")
        pThi_ready = sem("pThi_ready")
        pTlo_ready = sem("pTlo_ready")
        ctx_ps = sem("ctx_ps")
        rsum_ready = sem("rsum_ready")
        ctx_free = sem("ctx_free")
        chi_ready = sem("chi_ready")
        clo_ready = sem("clo_ready")
        cT_ps = sem("cT_ps")
        cThi_ready = sem("cThi_ready")
        cTlo_ready = sem("cTlo_ready")
        attn_ps = sem("attn_ps")
        stored = sem("stored")
        dve_step = sem("dve_step")

        block = ctx.enter_context(nc.Block())

        def weight_splits():
            for n, wT in enumerate((w1T, w3T)):
                for c in range(DC):
                    yield bank[2 * n + c][:, 0:EF], [t[:, c, :] for t in wT]
            yield bank[4][:, 0:2 * D], [t[:, 0:2, :].rearrange("p j d -> p (j d)") for t in w2T]
            yield bank[5][:, 0:D], [t[:, 2, :] for t in w2T]
            src = bank[5][:, D:D + DC * LAT].rearrange("p (c l) -> p c l", c=DC)
            yield src.unsqueeze(2).to_broadcast([P, DC, 2, LAT]), [t[:, :, :, :] for t in wdT]
        N_W = 2 * DC + 3
        GATE_AT = D + DC * LAT

        def tokens(t):
            return slice(t * HALF, (t + 1) * HALF)

        def blk(n):
            return slice(n * P, (n + 1) * P)

        def beyond(i, j):
            return isinstance(i, int) and i * UNITS + j >= NP * UNITS

        @block.sync
        def _(sp):
            sp.dma_start(X[:, 0:HB, :], x_d[:, 0:HB, :]).then_inc(ld["x0"], 16)
            sp.dma_start(X[:, HB:NB, :], x_d[:, HB:NB, :]).then_inc(ld["x1"], 16)
            sp.dma_start(gaten[:, :], gate_w).then_inc(ld["gate"], 16)
            for c in range(DC):
                sp.dma_start(w2n[:, c, :].rearrange("p (e f) -> p e f", e=E),
                             w2[:, blk(c), :].rearrange("e p f -> p e f")).then_inc(ld["w2"], 16)
            sp.dma_start(wdn[:, :], W_down).then_inc(ld["wd"], 16)
            sp.dma_start(wq, W_q.rearrange("(h p) d -> p h d", p=P)).then_inc(ld["wq"], 16)
            sp.dma_start(wuk[:, :, :], W_uk.rearrange("(h p) l -> p h l", p=P)).then_inc(ld["wuk"], 16)
            sp.dma_start(wo, W_o.rearrange("(c p) n -> p c n", p=P)).then_inc(ld["wo"], 16)
            sp.dma_start(wuv[:, :, :], W_uv.rearrange("(h p) l -> p h l", p=P)).then_inc(ld["wuv"], 16)

            sp.wait_ge(woT_ready, 8)
            with sp.Fori(0, NP) as i:
                sp.wait_ge(u_lo, i * 2 + 2)
                for side in range(2):
                    for part in range(2):
                        sp.dma_start(uc[LAT * part:LAT * (part + 1), bass.ds(i * 2 + side, 1), :],
                                     stage[LAT * side:LAT * (side + 1), 0, part:part + 1, :]).then_inc(u_moved, 16)

            for n in range(NB):
                sp.wait_ge(x_added[2], n + 1)
                sp.dma_start(out_d[:, n, :], X[:, n, :]).then_inc(stored, 16)
            sp.wait_ge(stored, 16 * NB)

        @block.gpsimd
        def _(pool):
            nc.gpsimd.memset(ident[:, :], 0.0)
            nc.gpsimd.memset(tri[:, :], 1.0)
            nc.gpsimd.memset(onesb[:, :], 1.0)
            nc.gpsimd.memset(maskneg[:, :], 0.0)
            nc.gpsimd.memset(sel[:, :, :], 0.0)
            nc.gpsimd.memset(lat[:, :, LAT:LAT + 1], 1.0)
            nc.gpsimd.iota(rank_i[:, :, :], pattern=[[0, NB], [-1, E]], base=E, channel_multiplier=0).then_inc(const_step, 1)
            pool.wait_ge(const_step, 1)
            nc.gpsimd.affine_select(out=ident[:, :], in_=ident[:, :], compare_op=ALU.not_equal, fill=1.0,
                                    base=0, pattern=[[-1, P]], channel_multiplier=1)
            nc.gpsimd.affine_select(out=tri[:, :], in_=tri[:, :], compare_op=ALU.is_ge, fill=0.0,
                                    base=0, pattern=[[1, P]], channel_multiplier=-1)
            nc.gpsimd.affine_select(out=maskneg[:, :], in_=maskneg[:, :], compare_op=ALU.is_ge, fill=-1e30,
                                    base=0, pattern=[[-1, P]], channel_multiplier=1)
            nc.gpsimd.tensor_copy(rank[:, :, :], rank_i[:, :, :])
            nc.gpsimd.affine_select(out=sel[:, :, :], in_=sel[:, :, :], compare_op=ALU.not_equal, fill=1.0,
                                    base=0, pattern=[[EPC, FC], [1, EPC], [0, F]], channel_multiplier=-1).then_inc(const_step, 1)
            pool.wait_ge(const_step, 2)
            nc.gpsimd.tensor_copy(identb[:, :], ident[:, :])
            nc.gpsimd.affine_select(out=sel[:, :, :], in_=sel[:, :, :], compare_op=ALU.not_equal, fill=1.0,
                                    base=E, pattern=[[EPC, FC], [1, EPC], [0, F]], channel_multiplier=-1).then_inc(consts, 1)

            def ffn(L):
                k = 0
                for t in range(2):
                    for c in range(DC):
                        k += 1
                        pool.wait_ge(xThi_ready[2 * L], k)
                        nc.gpsimd.tensor_tensor(xT_lo[:, c, tokens(t)], xT[:, c, tokens(t)], xT_hi[:, c, tokens(t)],
                                                ALU.subtract).then_inc(xTlo_ready[2 * L], 1)
                for s in range(0, 2 * FC, 2):
                    t, j = divmod(s, FC)
                    pool.wait_ge(hThi_ready[L], s + 1)
                    nc.gpsimd.tensor_tensor(hT_lo[:, j, tokens(t)], g[:, j, tokens(t)], hT_hi[:, j, tokens(t)],
                                            ALU.subtract).then_inc(hTlo_pool[L], 1)

            ffn(0)
            pool.wait_ge(n_hi, 4)
            with pool.Fori(0, H) as h:
                for b in range(B):
                    pool.wait_ge(ctx_free, h * B + (B + b + 1))
                    nc.gpsimd.tensor_copy(c_hi[:, SB * b:SB * (b + 1), bass.ts(h, LAT)], cst[:, b, :, :]).then_inc(chi_ready, 1)
                    pool.wait_ge(chi_ready, h * B + (b + 1))
                    nc.gpsimd.tensor_tensor(c_lo[:, SB * b:SB * (b + 1), bass.ts(h, LAT)], cst[:, b, :, :],
                                            c_hi[:, SB * b:SB * (b + 1), bass.ts(h, LAT)], ALU.subtract).then_inc(clo_ready, 1)
            ffn(1)

        @block.scalar
        def _(act):
            act.dma_start(w1n[:, :, :], w1.rearrange("e f d -> (e f) d").rearrange("(j p) d -> p j d", p=P)).then_inc(ld["w1"], 16)
            act.dma_start(w3n[:, :, :], w3.rearrange("e f d -> (e f) d").rearrange("(j p) d -> p j d", p=P)).then_inc(ld["w3"], 16)

            def layernorm_std(i, t):
                act.wait_ge(var_ready[i], t + 1)
                half = slice(t * HB, (t + 1) * HB)
                nc.scalar.activation(std[:, half], ve[:, half], ACT.Sqrt).then_inc(std_ready[i], 1)

            def split_xT(L, t):
                for c in range(DC):
                    act.wait_ge(xT_32[L], DC * t + c + 1)
                    nc.scalar.copy(xT_hi[:, c, tokens(t)], xT[:, c, tokens(t)]).then_inc(xThi_ready[2 * L], 1)

            def ffn(L):
                def copy_h1(s):
                    act.wait_ge(h_ps[L], s + 1)
                    if s >= 2:
                        act.wait_ge(z_ready[L], s - 1)
                    nc.scalar.copy(h1c[:, s % 2, :], bank[2 * (s % 2)][:, :]).then_inc(h1_ready[L], 1)

                def silu(s):
                    t, j = divmod(s, FC)
                    act.wait_ge(z_ready[L], s + 1)
                    nc.scalar.activation(g[:, j, tokens(t)], g[:, j, tokens(t)], ACT.Silu).then_inc(silu_ready[L], 1)

                def split_h(s):
                    t, j = divmod(s, FC)
                    act.wait_ge(hw_ready[L], s + 1)
                    nc.scalar.copy(hT_hi[:, j, tokens(t)], g[:, j, tokens(t)]).then_inc(hThi_ready[L], 1)

                copy_h1(0)
                copy_h1(1)
                split_xT(L, 1)
                act.wait_ge(dlt_ready[L], 1)
                nc.scalar.activation(e2[:, :], dlt[:, :], ACT.Exp).then_inc(e2_ready[L], 1)
                silu(0)
                for s in range(2, 2 * FC - 1):
                    copy_h1(s)
                    silu(s - 1)
                split_h(0)
                copy_h1(5)
                silu(4)
                split_h(1)
                silu(5)
                for s in range(2, 2 * FC):
                    split_h(s)

            layernorm_std(0, 0)
            for k, (src, dst) in enumerate(weight_splits()):
                act.wait_ge(w_ps, N_W if k >= N_W - 2 else k + 1)
                nc.scalar.copy(dst[0], src).then_inc(w_hi, 1)
                if k == 2 * DC - 1:
                    split_xT(0, 0)
                    layernorm_std(0, 1)
            ffn(0)

            for k in range(4):
                act.wait_ge(m_ps, k + 1)
                c, hg = divmod(k, 2)
                nc.scalar.activation(Mq[0][:, c, 8 * hg:8 * hg + 8, :].rearrange("p h l -> p (h l)"), bank[4 + k][:, :],
                                     ACT.Copy, scale=SCALE).then_inc(m_hi, 1)
            layernorm_std(1, 0)
            layernorm_std(1, 1)
            for k in range(8):
                act.wait_ge(woT_ps, k + 1)
                nc.scalar.copy(woT[:, 2 * k:2 * k + 2, :].rearrange("p h d -> p (h d)"), bank[k % 4][:, :]).then_inc(woT_ready, 1)
            for k in range(4):
                act.wait_ge(n_ps, k + 1)
                nc.scalar.copy(Nv[0][:, 2 * k:2 * k + 2, :].rearrange("p h d -> p (h d)"), bank[4 + k][:, :]).then_inc(n_hi, 1)
            for k in range(2 * DC):
                t, c = divmod(k, DC)
                act.wait_ge(xT_ps[1], k + 1)
                nc.scalar.copy(xT_hi[:, c, tokens(t)], bank[k][:, :]).then_inc(xThi_ready[1], 1)
            for t in range(2):
                act.wait_ge(lat_ps, t + 1)
                nc.scalar.copy(latT_hi[:, tokens(t)], bank[4 + t][:, :]).then_inc(lat_hi, 1)
            act.wait_ge(lat_ps, 3)
            nc.scalar.copy(lat[:, :, 0:LAT], bank[6][:, :].rearrange("p (n l) -> p n l", n=NB)).then_inc(lat_hi, 1)

            def split_queries(i, t):
                if not isinstance(i, int):
                    act.wait_ge(u_moved, i * 64)
                act.wait_ge(u_ps, i * 2 + (t + 1))
                nc.scalar.copy(stage[:, 0, 0, tokens(t)], bank[7][:, :]).then_inc(u_hi, 1)

            def exponent(i, j):
                u = j % UNITS
                act.wait_ge(max_ready, i * UNITS + (j + 1))
                for n, (b, q, at) in enumerate(HEAD_UNITS[u % HU]):
                    cols = slice(at, at + P * (q + 1))
                    last = nc.scalar.activation(prob[:, u % 2, cols], bank[SCORE_BANK[u]][:, cols], ACT.Exp,
                                                bias=nmax[:, u, n:n + 1])
                last.then_inc(prob_ready, 1)

            def split(i, j):
                act.wait_ge(pT_ps, i * UNITS + (j + 1))
                nc.scalar.copy(pT_hi[:, j % 2, :], bank[3 + j % 2][:, :]).then_inc(pThi_ready, 1)

            def attention_step(i, j, queries=True):
                if not beyond(i, j + 3):
                    exponent(i, j + 3)
                if not beyond(i, j + 2):
                    split(i, j + 2)
                if queries and j in (1, 2):
                    split_queries(i + 1, j - 1)

            for t in range(2):
                split_queries(0, t)
            exponent(0, 0)
            exponent(0, 1)
            split(0, 0)
            exponent(0, 2)
            split(0, 1)
            attention_step(0, 0)
            with act.Fori(0, NP - 1) as i:
                for j in range(1, UNITS + 1):
                    attention_step(i, j)
            for j in range(1, UNITS):
                attention_step(NP - 1, j, queries=False)

            def context_hi(r, waited):
                act.wait_ge(cT_ps, waited)
                nc.scalar.copy(stage[:, r, 0, :], bank[2 * r][:, :].bitcast(BF16)).then_inc(cThi_ready, 1)

            context_hi(0, 1)
            with act.Fori(0, NB // 2 - 1) as i:
                context_hi(1, i * 2 + 2)
                context_hi(0, i * 2 + 3)
            context_hi(1, NB)
            layernorm_std(2, 0)
            split_xT(1, 0)
            layernorm_std(2, 1)
            ffn(1)

        @block.vector
        def _(dve):
            steps = [0]

            def link(ins):
                steps[0] += 1
                ins.then_inc(dve_step, 1)
                dve.wait_ge(dve_step, steps[0])

            def variances(i, t):
                half = range(HB * t, HB * (t + 1))
                if i == 0:
                    dve.wait_ge(ld[f"x{t}"], 16)
                for n in half:
                    last = nc.vector.bn_stats(st[:, n, :], X[:, n, :])
                link(last)
                for n in half:
                    last = nc.vector.bn_aggr(mv[:, n, :], st[:, n, :])
                link(last)
                nc.vector.tensor_scalar_add(ve[:, HB * t:HB * (t + 1)], mv[:, HB * t:HB * (t + 1), 1], EPS).then_inc(var_ready[i], 1)

            def normalise_tokens(i, t):
                dve.wait_ge(std_ready[i], t + 1)
                link(nc.vector.reciprocal(rstd[:, HB * t:HB * (t + 1)], std[:, HB * t:HB * (t + 1)]))
                for n in range(HB * t, HB * (t + 1)):
                    nc.vector.tensor_scalar(xn[:, n, :], X[:, n, :], mv[:, n, 0:1], rstd[:, n:n + 1],
                                            ALU.subtract, ALU.mult).then_inc(xn_ready[i], 1)

            def copy_xT(L, t):
                for c in range(DC):
                    dve.wait_ge(xT_ps[2 * L], DC * t + c + 1)
                    nc.vector.tensor_copy(xT[:, c, tokens(t)], bank[6 - 2 * t + c][:, :]).then_inc(xT_32[L], 1)

            def split_weights(ks):
                for k, (src, dst) in enumerate(weight_splits()):
                    if k in ks:
                        dve.wait_ge(w_hi, N_W if k >= N_W - 2 else k + 1)
                        nc.vector.tensor_tensor(dst[1], src, dst[0], ALU.subtract).then_inc(w_lo, 1)

            def over_experts(v):
                return v.unsqueeze(2).to_broadcast([P, NB, E])

            def choose(src, k):
                link(nc.vector.reduce_max(top[:, k, :], src, AX.X))
                link(nc.vector.tensor_tensor(eq[:, :, :], src, over_experts(top[:, k, :]), ALU.is_equal))
                link(nc.vector.tensor_tensor(tb[:, :, :], eq[:, :, :], rank[:, :, :], ALU.mult))
                link(nc.vector.reduce_max(tr[:, k, :], tb[:, :, :], AX.X))
                link(nc.vector.tensor_tensor(chosen[:, k, :, :], tb[:, :, :], over_experts(tr[:, k, :]), ALU.is_equal))

            def ffn(L):
                def product(s):
                    t, j = divmod(s, FC)
                    dve.wait_ge(h1_ready[L], s + 1)
                    nc.vector.tensor_tensor(g[:, j, tokens(t)], h1c[:, s % 2, :], bank[2 * (s % 2) + 1][:, :],
                                            ALU.mult).then_inc(z_ready[L], 1)

                def weigh(s):
                    t, j = divmod(s, FC)
                    dve.wait_ge(wexp_ps[L], s + 1)
                    dve.wait_ge(silu_ready[L], s + 1)
                    nc.vector.tensor_tensor(g[:, j, tokens(t)], g[:, j, tokens(t)], bank[5 + 2 * (s % 2)][:, :],
                                            ALU.mult).then_inc(hw_ready[L], 1)

                def split_h(s):
                    t, j = divmod(s, FC)
                    dve.wait_ge(hThi_ready[L], s + 1)
                    nc.vector.tensor_tensor(hT_lo[:, j, tokens(t)], g[:, j, tokens(t)], hT_hi[:, j, tokens(t)],
                                            ALU.subtract).then_inc(hTlo_dve[L], 1)

                product(0)
                dve.wait_ge(lg_ps[L], 1)
                link(nc.vector.tensor_copy(lg[:, :, :], bank[6][:, 0:NB * E].rearrange("p (n e) -> p n e", n=NB)))
                choose(lg[:, :, :], 0)
                link(nc.vector.tensor_scalar(cp[:, :, :], chosen[:, 0, :, :], -0.5, -2.0 * HUGE, ALU.add, ALU.mult))
                link(nc.vector.tensor_tensor(l2[:, :, :], lg[:, :, :], cp[:, :, :], ALU.min))
                choose(l2[:, :, :], 1)
                nc.vector.tensor_tensor(dlt[:, :], top[:, 1, :], top[:, 0, :], ALU.subtract).then_inc(dlt_ready[L], 1)
                dve.wait_ge(dlt_ready[L], 1)

                product(1)

                dve.wait_ge(e2_ready[L], 1)
                link(nc.vector.tensor_scalar_add(den[:, :], e2[:, :], 1.0))
                link(nc.vector.reciprocal(rec[:, :], den[:, :]))
                nc.vector.tensor_scalar(rw[:, 0, :], rec[:, :], 0.5, None, ALU.mult)
                link(nc.vector.scalar_tensor_tensor(out=rw[:, 1, :], in0=rec[:, :], scalar=0.5, in1=e2[:, :],
                                                    op0=ALU.mult, op1=ALU.mult))
                dve.wait_ge(pos_ps[L], 1)
                link(nc.vector.scalar_tensor_tensor(
                    out=kept[:, :, :, :].rearrange("p s n e -> p (s n e)"), in0=bank[5][:, 0:2 * NB * E],
                    scalar=float(CAP), in1=chosen[:, :, :, :].rearrange("p s n e -> p (s n e)"),
                    op0=ALU.is_le, op1=ALU.mult))
                for k in range(2):
                    last = nc.vector.tensor_tensor(kept[:, k, :, :], kept[:, k, :, :], over_experts(rw[:, k, :]), ALU.mult)
                link(last)
                link(nc.vector.tensor_tensor(wgt[:, :, :], kept[:, 0, :, :], kept[:, 1, :, :], ALU.add))
                link(nc.vector.tensor_copy(wgt_hl[:, :, 0, :], wgt[:, :, :]))
                nc.vector.tensor_tensor(wgt_hl[:, :, 1, :], wgt[:, :, :], wgt_hl[:, :, 0, :],
                                        ALU.subtract).then_inc(wgt_ready[L], 1)
                product(2)
                product(3)
                dve.wait_ge(wgtT_ps[L], 1)
                nc.vector.tensor_copy(wgtT[:, :], bank[6][0:2 * E, :].bitcast(BF16)).then_inc(wgtT_ready[L], 1)
                product(4)
                weigh(0)
                weigh(1)
                product(5)
                weigh(2)
                split_h(1)
                weigh(3)
                weigh(4)
                split_h(3)
                weigh(5)
                split_h(5)
                for n in range(NB):
                    dve.wait_ge(y_ps[L], n + 1)
                    nc.vector.tensor_tensor(X[:, n, :], X[:, n, :], bank[n % 4][:, 0:D], ALU.add).then_inc(x_added[2 * L], 1)
                dve.wait_ge(x_added[2 * L], NB)

            variances(0, 0)
            normalise_tokens(0, 0)
            split_weights(range(2 * DC))
            copy_xT(0, 0)
            variances(0, 1)
            normalise_tokens(0, 1)
            split_weights(range(2 * DC, N_W))
            nc.vector.tensor_copy(gateT[:, :, :], bank[5][:, GATE_AT:GATE_AT + DC * E].rearrange("p (c e) -> p c e", c=DC)).then_inc(w_lo, 1)
            copy_xT(0, 1)
            dve.wait_ge(consts, 1)
            ffn(0)

            variances(1, 0)
            variances(1, 1)
            for k in range(4):
                dve.wait_ge(m_hi, k + 1)
                c, hg = divmod(k, 2)
                hi, lo = (m[:, c, 8 * hg:8 * hg + 8, :].rearrange("p h l -> p (h l)") for m in Mq)
                nc.vector.scalar_tensor_tensor(out=lo, in0=bank[4 + k][:, :], scalar=SCALE, in1=hi,
                                               op0=ALU.mult, op1=ALU.subtract).then_inc(m_lo, 1)
            normalise_tokens(1, 0)
            normalise_tokens(1, 1)
            for k in range(4):
                dve.wait_ge(n_hi, k + 1)
                hi, lo = (m[:, 2 * k:2 * k + 2, :].rearrange("p h d -> p (h d)") for m in Nv)
                nc.vector.tensor_tensor(lo, bank[4 + k][:, :], hi, ALU.subtract).then_inc(n_lo, 1)
            for k in range(2 * DC):
                t, c = divmod(k, DC)
                dve.wait_ge(xThi_ready[1], k + 1)
                nc.vector.tensor_tensor(xT_lo[:, c, tokens(t)], bank[k][:, :], xT_hi[:, c, tokens(t)],
                                        ALU.subtract).then_inc(xTlo_ready[1], 1)
            for t in range(2):
                dve.wait_ge(lat_hi, t + 1)
                nc.vector.tensor_tensor(latT_lo[:, tokens(t)], bank[4 + t][:, :], latT_hi[:, tokens(t)],
                                        ALU.subtract).then_inc(lat_lo, 1)
            dve.wait_ge(lat_hi, 3)
            nc.vector.tensor_tensor(lat[:, :, LAT + 1:2 * LAT + 1], bank[6][:, :].rearrange("p (n l) -> p n l", n=NB),
                                    lat[:, :, 0:LAT], ALU.subtract).then_inc(lat_lo, 1)

            def split_queries(i, t):
                dve.wait_ge(u_hi, i * 2 + (t + 1))
                nc.vector.tensor_tensor(stage[:, 0, 1, tokens(t)], bank[7][:, :], stage[:, 0, 0, tokens(t)],
                                        ALU.subtract).then_inc(u_lo, 1)

            def row_max(i, j):
                u = j % UNITS
                dve.wait_ge(s_ps, i * UNITS + (j + 1))
                parts = HEAD_UNITS[u % HU]
                src = bank[SCORE_BANK[u]]
                if len({q for _, q, _ in parts}) == 1:
                    last = nc.vector.tensor_reduce(nmax[:, u, 0:len(parts)], src[:, :].rearrange("p (a n) -> p a n", a=len(parts)),
                                                   AX.X, ALU.max, negate=True)
                else:
                    for n, (b, q, at) in enumerate(parts):
                        last = nc.vector.tensor_reduce(nmax[:, u, n:n + 1], src[:, at:at + P * (q + 1)], AX.X, ALU.max, negate=True)
                last.then_inc(max_ready, 1)

            def split(i, j):
                dve.wait_ge(pThi_ready, i * UNITS + (j + 1))
                nc.vector.tensor_tensor(pT_lo[:, j % 2, :], bank[3 + j % 2][:, :], pT_hi[:, j % 2, :],
                                        ALU.subtract).then_inc(pTlo_ready, 1)

            def normalise(i, side, b):
                src = bank[5 + b][:, 0:SB * (LAT + 1)].rearrange("p (q l) -> p q l", q=SB)
                dve.wait_ge(ctx_ps, i * (2 * B) + (side * B + b + 1))
                nc.vector.reciprocal(rsum[:, b, :], src[:, :, LAT]).then_inc(rsum_ready, 1)
                if not (isinstance(i, int) and i == 0 and side == 0):
                    dve.wait_ge(clo_ready, i * (2 * B) + side * B)
                dve.wait_ge(rsum_ready, i * (2 * B) + (side * B + b + 1))
                nc.vector.tensor_tensor(cst[:, b, :, :], src[:, :, 0:LAT],
                                        rsum[:, b, :].unsqueeze(2).to_broadcast([P, SB, LAT]), ALU.mult).then_inc(ctx_free, 1)

            def attention_step(i, j, queries=True):
                if not beyond(i, j + 1):
                    split(i, j + 1)
                if not beyond(i, j + 4):
                    row_max(i, j + 4)
                if queries and j in (1, 2):
                    split_queries(i + 1, j - 1)
                side, unit = divmod(j - 1, HU)
                if j and unit in SEQ_DONE:
                    normalise(i, side, SEQ_DONE[unit])

            for t in range(2):
                split_queries(0, t)
            nc.vector.memset(rsum[:, :, :], 0.0).then_inc(ctx_free, B)
            for j in range(4):
                row_max(0, j)
            split(0, 0)
            attention_step(0, 0)
            with dve.Fori(0, NP - 1) as i:
                for j in range(1, UNITS + 1):
                    attention_step(i, j)
            for j in range(1, UNITS + 1):
                attention_step(NP - 1, j, queries=False)

            def context_lo(r, waited):
                dve.wait_ge(cThi_ready, waited)
                nc.vector.tensor_copy(stage[:, r, 1, :], bank[2 * r + 1][:, :].bitcast(BF16)).then_inc(cTlo_ready, 1)

            def add_attention(r, n, waited):
                dve.wait_ge(attn_ps, waited)
                nc.vector.tensor_tensor(X[:, bass.ds(n, 1), :], X[:, bass.ds(n, 1), :],
                                        bank[4 + r][:, 0:D].unsqueeze(1), ALU.add).then_inc(x_added[1], 1)

            context_lo(0, 1)
            with dve.Fori(0, NB // 2 - 1) as i:
                context_lo(1, i * 2 + 2)
                add_attention(0, i * 2, i * 2 + 1)
                context_lo(0, i * 2 + 3)
                add_attention(1, i * 2 + 1, i * 2 + 2)
            dve.wait_ge(x_added[1], NB - 2)
            variances(2, 0)
            context_lo(1, NB)
            add_attention(0, NB - 2, NB - 1)
            normalise_tokens(2, 0)
            copy_xT(1, 0)
            add_attention(1, NB - 1, NB)
            dve.wait_ge(x_added[1], NB)
            variances(2, 1)
            normalise_tokens(2, 1)
            copy_xT(1, 1)
            ffn(1)

        @block.tensor
        def _(pe):
            mm = nc.tensor.matmul

            def split_product(dst, left, right, K, start=True, stop=True):
                terms = [(0, 0, k) for k in range(K)] + [(0, 1, k) for k in range(K)] + [(1, 0, k) for k in range(K)]
                for n, (a, b, k) in enumerate(terms):
                    last = mm(dst, left(k)[a], right(k)[b], start=start and n == 0, stop=stop and n == len(terms) - 1)
                return last

            def transpose_xn(i, t, banks):
                pe.wait_ge(xn_ready[i], HB * (t + 1))
                for c in range(DC):
                    for n in range(HB):
                        last = nc.tensor.transpose(bank[banks + c][:, blk(n)], xn[:, HB * t + n, blk(c)], ident[:, :])
                    last.then_inc(xT_ps[i], 1)

            def ffn(L):
                def hidden(s):
                    t, j = divmod(s, FC)
                    pe.wait_ge(xThi_ready[2 * L], DC * (t + 1))
                    if s >= 2:
                        pe.wait_ge(z_ready[L], s - 1)
                    for part, wparts in ((0, (0, 1)), (1, (0,))):
                        if part:
                            pe.wait_ge(xTlo_ready[2 * L], DC * (t + 1))
                        for n, wT in enumerate((w1T, w3T)):
                            for w in wparts:
                                for k in range(DC):
                                    last = mm(bank[2 * (s % 2) + n][:, :], wT[w][:, k, blk(j)], (xT_hi, xT_lo)[part][:, k, tokens(t)],
                                              start=(part == 0 and w == 0 and k == 0), stop=(part == 1 and k == DC - 1))
                    last.then_inc(h_ps[L], 1)

                def spread(s):
                    t, j = divmod(s, FC)
                    if s >= 2:
                        pe.wait_ge(hw_ready[L], s - 1)
                    mm(bank[5 + 2 * (s % 2)][:, :], sel[:, j, :], wgtT[:, tokens(t)], start=True, stop=True).then_inc(wexp_ps[L], 1)

                if L == 0:
                    pe.wait_ge(w_lo, 2 * DC)
                hidden(0)
                hidden(1)
                if L == 0:
                    pe.wait_ge(w_lo, N_W + 1)
                else:
                    pe.wait_ge(x_added[1], NB)
                transpose_xn(2 * L, 1, 4)
                pe.wait_ge(xT_32[L], 2 * DC)
                for n in range(NB):
                    for c in range(DC):
                        last = mm(bank[6][:, n * E:(n + 1) * E], xT[:, c, blk(n)], gateT[:, c, :], start=(c == 0), stop=(c == DC - 1))
                last.then_inc(lg_ps[L], 1)
                hidden(2)
                pe.wait_ge(dlt_ready[L], 1)
                picks = chosen[:, :, :, :].rearrange("p s n e -> p (s n e)")
                G = 2 * NB
                mm(bank[5][:, 0:G * E], tri[:, :], picks, start=True, stop=False)
                for k in range(1, G):
                    last = mm(bank[5][:, k * E:G * E], onesb[:, :], picks[:, 0:(G - k) * E], start=False, stop=(k == G - 1))
                last.then_inc(pos_ps[L], 1)
                hidden(3)
                pe.wait_ge(wgt_ready[L], 1)
                for n in range(NB):
                    last = nc.tensor.transpose(bank[6][0:2 * E, :].bitcast(BF16)[:, blk(n)],
                                               wgt_hl[:, n, :, :].rearrange("p a e -> p (a e)"), identb[:, :])
                last.then_inc(wgtT_ps[L], 1)
                hidden(4)
                pe.wait_ge(wgtT_ready[L], 1)
                spread(0)
                spread(1)
                hidden(5)
                for s in range(2, 2 * FC):
                    spread(s)
                pe.wait_ge(z_ready[L], 2 * FC)
                for n in range(NB):
                    t = n // HB
                    pe.wait_ge(hThi_ready[L], FC * (t + 1))
                    if n >= 4:
                        pe.wait_ge(x_added[2 * L], n - 3)
                    for part, wparts in ((0, (0, 1)), (1, (0,))):
                        if part:
                            pe.wait_ge(hTlo_pool[L], (2, 3)[t])
                            pe.wait_ge(hTlo_dve[L], (1, 3)[t])
                        for w in wparts:
                            for k in range(FC):
                                last = mm(bank[n % 4][:, 0:D], (hT_hi, hT_lo)[part][:, k, blk(n)], w2T[w][:, k, :],
                                          start=(part == 0 and w == 0 and k == 0), stop=(part == 1 and k == FC - 1))
                    last.then_inc(y_ps[L], 1)

            pe.wait_ge(consts, 1)
            for n, (wn, key) in enumerate(((w1n, "w1"), (w3n, "w3"))):
                pe.wait_ge(ld[key], 16)
                for c in range(DC):
                    for j in range(FC):
                        last = nc.tensor.transpose(bank[2 * n + c][:, blk(j)], wn[:, j, blk(c)], ident[:, :])
                    last.then_inc(w_ps, 1)
            transpose_xn(0, 0, 6)
            pe.wait_ge(ld["w2"], 16 * DC)
            for j in range(FC):
                for c in range(DC):
                    at = (j % 2) * D + c * P
                    last = nc.tensor.transpose(bank[4 + j // 2][:, at:at + P], w2n[:, c, blk(j)], ident[:, :])
                if j >= 1:
                    last.then_inc(w_ps, 1)
            pe.wait_ge(ld["gate"], 16)
            pe.wait_ge(ld["wd"], 16)
            for c in range(DC):
                nc.tensor.transpose(bank[5][:, GATE_AT + c * E:GATE_AT + (c + 1) * E], gaten[:, blk(c)], ident[0:E, 0:E])
            for c in range(DC):
                last = nc.tensor.transpose(bank[5][:, D + c * LAT:D + (c + 1) * LAT], wdn[:, blk(c)], ident[0:LAT, 0:LAT])
            last.then_inc(w_ps, 1)
            ffn(0)

            pe.wait_ge(ld["wq"], 16)
            pe.wait_ge(ld["wuk"], 16)
            for k in range(4):
                c, hg = divmod(k, 2)
                for h in range(8):
                    last = mm(bank[4 + k][:, LAT * h:LAT * (h + 1)], wq[:, 8 * hg + h, blk(c)], wuk[:, 8 * hg + h, :], start=True, stop=True)
                last.then_inc(m_ps, 1)
            pe.wait_ge(x_added[0], NB)
            pe.wait_ge(ld["wo"], 16)
            for k in range(8):
                if k >= 4:
                    pe.wait_ge(woT_ready, k - 3)
                for h in range(2):
                    for c in range(DC):
                        at = D * h + P * c
                        last = nc.tensor.transpose(bank[k % 4][:, at:at + P], wo[:, c, blk(2 * k + h)], ident[:, :])
                last.then_inc(woT_ps, 1)
            pe.wait_ge(ld["wuv"], 16)
            for k in range(4):
                pe.wait_ge(m_lo, k + 1)
                pe.wait_ge(woT_ready, 2 * k + 2)
                for h in range(4):
                    side = h % 2
                    last = mm(bank[4 + k][LAT * side:LAT * (side + 1), D * (h // 2):D * (h // 2 + 1)],
                              wuv[:, 4 * k + h, :], woT[:, 4 * k + h, :], start=True, stop=True)
                last.then_inc(n_ps, 1)

            pe.wait_ge(woT_ready, 8)
            for t in range(2):
                transpose_xn(1, t, DC * t)
            for t in range(2):
                pe.wait_ge(n_lo, t + 1)
                pe.wait_ge(xTlo_ready[1], DC * (t + 1))
                split_product(bank[4 + t][:, :],
                              lambda k: [w[:, k, :, :].rearrange("p r l -> p (r l)") for w in wdT],
                              lambda k: [xT_hi[:, k, tokens(t)], xT_lo[:, k, tokens(t)]], DC).then_inc(lat_ps, 1)
            pe.wait_ge(n_lo, 3)
            for n in range(NB):
                last = split_product(bank[6][:, LAT * n:LAT * (n + 1)],
                                     lambda k: [xT_hi[:, k, blk(n)], xT_lo[:, k, blk(n)]],
                                     lambda k: [w[:, k, 0, :] for w in wdT], DC)
            last.then_inc(lat_ps, 1)

            def queries(i, t):
                if not (isinstance(i, int) and t == 0):
                    pe.wait_ge(u_lo, i * 2 + t)
                split_product(bank[7][:, :],
                              lambda k: [m[:, k, bass.ds(i * 2, 2), :].rearrange("p h l -> p (h l)") for m in Mq],
                              lambda k: [xT_hi[:, k, tokens(t)], xT_lo[:, k, tokens(t)]], DC).then_inc(u_ps, 1)

            def scores(i, j):
                u = j % UNITS
                if j == UNITS or (isinstance(i, int) and i + j == 0):
                    pe.wait_ge(u_moved, i * 64 + 64 * (j // UNITS + 1))
                held = HELD_BY[u] + j - u
                if not (isinstance(i, int) and i * UNITS + held < 0):
                    pe.wait_ge(prob_ready, i * UNITS + (held + 1))
                dst = bank[SCORE_BANK[u]]
                for n, (b, q, at) in enumerate(HEAD_UNITS[u % HU]):
                    cols = slice(at, at + P * (q + 1))
                    keys = slice(SEQ * b, SEQ * b + P * (q + 1))
                    queries_of = uc[:, i * 2 + j // HU, SEQ * b + P * q:SEQ * b + P * (q + 1)]
                    mm(dst[:, cols], queries_of, latT_hi[:, keys], start=True, stop=False)
                    mm(dst[:, cols], queries_of, latT_lo[:, keys], start=False, stop=False)
                    last = mm(dst[:, cols][:, P * q:], identb[:, :], maskneg[:, :], start=False, stop=True)
                last.then_inc(s_ps, 1)

            def transposes(i, j):
                pe.wait_ge(prob_ready, i * UNITS + (j + 1))
                if not (isinstance(i, int) and i == 0 and j < 2):
                    pe.wait_ge(pTlo_ready, i * UNITS + (j - 1))
                for k in range(SB):
                    last = nc.tensor.transpose(bank[3 + j % 2][:, blk(k)], prob[:, j % 2, blk(k)], ident[:, :])
                last.then_inc(pT_ps, 1)

            def context(i, j):
                unit = j % HU
                if unit == 0 or unit == 2:
                    pe.wait_ge(ctx_free, i * (2 * B) + (j // HU * B + unit // 2 + 1))
                pe.wait_ge(pTlo_ready, i * UNITS + (j + 1))
                for b, q, at in HEAD_UNITS[unit]:
                    dst = bank[5 + b][:, q * (LAT + 1):(q + 1) * (LAT + 1)]
                    for k in range(q + 1):
                        n = SB * b + k
                        p_hi, p_lo = (p[:, j % 2, at + P * k:at + P * (k + 1)] for p in (pT_hi, pT_lo))
                        mm(dst, p_hi, lat[:, n, 0:LAT + 1], start=(k == 0), stop=False)
                        mm(dst[:, 0:LAT], p_hi, lat[:, n, LAT + 1:2 * LAT + 1], start=False, stop=False)
                        last = mm(dst, p_lo, lat[:, n, 0:LAT + 1], start=False, stop=(k == q))
                if unit in SEQ_DONE:
                    last.then_inc(ctx_ps, 1)

            def attention_step(i, j, with_queries=True):
                if not beyond(i, j + 4):
                    scores(i, j + 4)
                context(i, j)
                if not beyond(i, j + 2):
                    transposes(i, j + 2)
                if with_queries and j in (1, 2):
                    queries(i + 1, j - 1)

            queries(0, 0)
            queries(0, 1)
            pe.wait_ge(lat_lo, 3)
            pe.wait_ge(n_lo, 4)
            for j in range(3):
                scores(0, j)
            transposes(0, 0)
            scores(0, 3)
            transposes(0, 1)
            attention_step(0, 0)
            with pe.Fori(0, NP - 1) as i:
                for j in range(1, UNITS + 1):
                    attention_step(i, j)
            for j in range(1, UNITS):
                attention_step(NP - 1, j, with_queries=False)

            pe.wait_ge(clo_ready, B * H)

            def transpose_context(r, n):
                for part, src in enumerate((c_hi, c_lo)):
                    for k in range(NP):
                        last = nc.tensor.transpose(bank[2 * r + part][:, :].bitcast(BF16)[:, blk(k)], src[:, n, blk(k)], identb[:, :])
                last.then_inc(cT_ps, 1)

            def project(r, waited):
                pe.wait_ge(cTlo_ready, waited)
                split_product(bank[4 + r][:, 0:D],
                              lambda k: [stage[:, r, part, blk(k)] for part in range(2)],
                              lambda k: [m[:, k, :] for m in Nv], NP).then_inc(attn_ps, 1)

            transpose_context(0, 0)
            with pe.Fori(0, NB // 2 - 1) as i:
                transpose_context(1, i * 2 + 1)
                project(0, i * 2 + 1)
                transpose_context(0, i * 2 + 2)
                project(1, i * 2 + 2)
            transpose_context(1, NB - 1)
            project(0, NB - 1)
            project(1, NB)
            transpose_xn(2, 0, 6)
            ffn(1)


_INS = ['L0_attn_x', 'L0_attn_W_down', 'L0_attn_W_uk', 'L0_attn_W_uv', 'L0_attn_W_q', 'L0_attn_W_o',
        'L0_ffn_gate_w', 'L0_ffn_w1', 'L0_ffn_w2', 'L0_ffn_w3']
_OUTS = [((2, 512, 256), 'float32')]


def kernel(**inputs):
    import numpy as _np
    import concourse.bacc as _bacc
    from concourse import mybir as _mybir
    from concourse.bass_utils import run_bass_kernel_spmd as _run

    nc = _bacc.Bacc("TRN2", target_bir_lowering=False, num_devices=1)
    arrays, args = {}, []
    for name in _INS:
        a = _np.ascontiguousarray(inputs[name])
        arrays[f"in_{name}_dram"] = a
        args.append(nc.dram_tensor(f"in_{name}_dram", a.shape, _mybir.dt.from_np(a.dtype), kind="ExternalInput").ap())
    for i, (shape, dtype) in enumerate(_OUTS):
        dt = _mybir.dt.from_np(_np.dtype(dtype))
        args.append(nc.dram_tensor(f"out_{i}_dram", shape, dt, kind="ExternalOutput").ap())
    bass_macaron_moe_mla_moe(nc, *args)
    r = _run(nc, [arrays], core_ids=[0])
    got = tuple(r.results[0][f"out_{i}_dram"] for i in range(len(_OUTS)))
    return got[0]
```

```python
import concourse.bass as bass
from concourse import mybir
from contextlib import ExitStack


def bass_macaron_moe_mla_moe(
    nc: bass.Bass,
    x_in: bass.AP,
    W_down: bass.AP,
    W_uk: bass.AP,
    W_uv: bass.AP,
    W_q: bass.AP,
    W_o: bass.AP,
    gate_w: bass.AP,
    w1: bass.AP,
    w2: bass.AP,
    w3: bass.AP,
    out: bass.AP,
):
    F32 = mybir.dt.float32
    BF16 = mybir.dt.bfloat16
    FP16 = mybir.dt.float16
    I32 = mybir.dt.int32
    ALU = mybir.AluOpType
    ACT = mybir.ActivationFunctionType
    AX = mybir.AxisListType

    P = 128
    B, SEQ, D = x_in.shape
    T = B * SEQ
    NB = T // P
    SB = SEQ // P
    DC = D // P
    HALF = T // 2
    HB = HALF // P
    E, F, _ = w1.shape
    EF = E * F
    FC = EF // P
    EPC = P // F
    CAP = -(-T * 5 // (E * 4))
    LAT = W_down.shape[0]
    H = W_uk.shape[0] // P
    NP = H // 2
    SCALE = 1.0 / float(P) ** 0.5
    EPS = 1e-5
    HUGE = 1.5e38
    HEAD_UNITS = [[(0, 2, 0), (0, 0, 3 * P)], [(0, 3, 0)], [(0, 1, 0), (1, 1, 2 * P)],
                  [(1, 2, 0), (1, 0, 3 * P)], [(1, 3, 0)]]
    HU = len(HEAD_UNITS)
    UNITS = 2 * HU
    LAST_UNIT = [2, 4]
    SCORE_BANK = [0, 1, 7, 2, 0, 1, 2, 0, 1, 7]
    HELD_BY = [-3, -2, -1, -4, 0, 1, 3, 4, 5, None]
    CTX_T_BANK = [(0, 7), (1, 2)]
    OUT_BANK = [3, 4]

    x_d = x_in.rearrange("b s d -> (b s) d").rearrange("(n p) d -> p n d", p=P)
    out_d = out.rearrange("b s d -> (b s) d").rearrange("(n p) d -> p n d", p=P)

    ctx = ExitStack()
    with ctx:
        def sb(name, shape, dt):
            return ctx.enter_context(nc.sbuf_tensor(name, shape, dt))

        def sem(name):
            return ctx.enter_context(nc.semaphore(name))

        ident = sb("ident", [P, P], F32)
        identb = sb("identb", [P, P], BF16)
        tri = sb("tri", [P, P], BF16)
        onesb = sb("onesb", [P, P], BF16)
        maskneg = sb("maskneg", [P, P], BF16)
        rank_i = sb("rank_i", [P, NB, E], I32)
        rank = sb("rank", [P, NB, E], F32)
        sel = sb("sel", [2 * E, FC, P], BF16)

        X = sb("X", [P, NB, D], F32)
        xn = sb("xn", [P, NB, D], F32)
        xT = sb("xT", [P, DC, HALF], F32)
        xT_hi = sb("xT_hi", [P, DC, T], FP16)
        xT_lo = sb("xT_lo", [P, DC, T], FP16)
        st = sb("st", [P, NB, 6], F32)
        mv = sb("mv", [P, NB, 2], F32)
        ve = sb("ve", [P, NB], F32)
        std = sb("std", [P, NB], F32)
        rstd = sb("rstd", [P, NB], F32)

        ffn_buf = sb("ffn_buf", [P, 4, T], F32)
        g = ffn_buf[:, 0:FC, :]
        h1c = ffn_buf[:, FC, :].rearrange("p (b n) -> p b n", b=2)
        hT_hi = sb("hT_hi", [P, FC, T], BF16)
        hT_lo = sb("hT_lo", [P, FC, T], BF16)
        lg = sb("lg", [P, NB, E], F32)
        eq = sb("eq", [P, NB, E], F32)
        tb = sb("tb", [P, NB, E], F32)
        cp = sb("cp", [P, NB, E], F32)
        l2 = sb("l2", [P, NB, E], F32)
        top = sb("top", [P, 2, NB], F32)
        tr = sb("tr", [P, 2, NB], F32)
        dlt = sb("dlt", [P, NB], F32)
        e2 = sb("e2", [P, NB], F32)
        den = sb("den", [P, NB], F32)
        rec = sb("rec", [P, NB], F32)
        rw = sb("rw", [P, 2, NB], F32)
        chosen = sb("chosen", [P, 2, NB, E], BF16)
        kept = sb("kept", [P, 2, NB, E], F32)
        wgt = sb("wgt", [P, NB, E], F32)
        wgt_hl = sb("wgt_hl", [P, NB, 2, E], BF16)
        wgtT = sb("wgtT", [2 * E, T], BF16)

        w1n = sb("w1n", [P, FC, D], F32)
        w3n = sb("w3n", [P, FC, D], F32)
        w2n = sb("w2n", [P, DC, EF], F32)
        gaten = sb("gaten", [E, D], F32)
        wdn = sb("wdn", [LAT, D], F32)
        gateT = sb("gateT", [P, DC, E], F32)
        gate_rest = sb("gate_rest", [P, DC, E], F32)
        gate_parts = sb("gate_parts", [P, DC, 3, E], BF16)
        w1T = [sb("w1T_hi", [P, DC, EF], BF16), sb("w1T_lo", [P, DC, EF], BF16)]
        w3T = [sb("w3T_hi", [P, DC, EF], BF16), sb("w3T_lo", [P, DC, EF], BF16)]
        w2T = [sb("w2T_hi", [P, FC, D], BF16), sb("w2T_lo", [P, FC, D], BF16)]
        wdT = [sb("wdT_hi", [P, DC, 2, LAT], BF16), sb("wdT_lo", [P, DC, 2, LAT], BF16)]
        wuk = sb("wuk", [P, H, LAT], F32)
        wuv = sb("wuv", [P, H, LAT], F32)
        wqo = sb("wqo", [P, 2, H * D], F32)
        wq = wqo[:, 0, :].rearrange("p (h d) -> p h d", h=H)
        wo = wqo[:, 1, :].rearrange("p (c n) -> p c n", c=DC)
        uc = wqo[:, :, :].rearrange("p a n -> p (a n)").bitcast(BF16).rearrange("p (h t) -> p h t", h=H)
        woT_buf = sb("woT_buf", [P, 2, H * D], BF16)
        woT = [woT_buf[:, part, :].rearrange("p (h d) -> p h d", h=H) for part in range(2)]
        c_hi = woT_buf[:, :, :].rearrange("p a n -> p (a n)").rearrange("p (n c) -> p n c", n=NB)
        wuv_hl = [sb("wuv_hi", [P, H, LAT], BF16), sb("wuv_lo", [P, H, LAT], BF16)]
        c_lo = ffn_buf[:, :, :].rearrange("p a n -> p (a n)").bitcast(BF16).rearrange("p (n c) -> p n c", n=NB)
        Mq = [sb("Mq_hi", [P, DC, H, LAT], BF16), sb("Mq_lo", [P, DC, H, LAT], BF16)]
        Nv = [sb("Nv_hi", [P, NP, D], BF16), sb("Nv_lo", [P, NP, D], BF16)]

        latT_hi = sb("latT_hi", [P, T], BF16)
        latT_lo = sb("latT_lo", [P, T], BF16)
        lat = sb("lat", [P, NB, 2 * LAT + 1], BF16)
        stage = sb("stage", [P, 2, 2, T], BF16)
        prob = sb("prob", [P, 2, SEQ], F32)
        pT_hi = sb("pT_hi", [P, 2, SEQ], FP16)
        pT_lo = sb("pT_lo", [P, 2, SEQ], FP16)
        nmax = sb("nmax", [P, UNITS, 2], F32)
        rsum = sb("rsum", [P, B, SB], F32)
        craw = sb("craw", [P, B, SB, LAT], F32)
        cst = sb("cst", [P, B, SB, LAT], F32)

        bank = [ctx.enter_context(nc.psum_tensor(f"bank{i}", [P, 512], F32)) for i in range(8)]

        ld = {n: sem(f"ld_{n}") for n in ("x0", "x1", "gate", "w1", "w3", "w2", "wd", "wq", "wuk", "wuv", "wo")}
        consts = sem("consts")
        ones_ready = sem("ones_ready")
        const_step = sem("const_step")
        var_ready = [sem(f"var_ready{i}") for i in range(3)]
        st_ready = sem("st_ready")
        std_ready = [sem(f"std_ready{i}") for i in range(3)]
        xn_ready = [sem(f"xn_ready{i}") for i in range(3)]
        xT_ps = [sem(f"xT_ps{i}") for i in range(3)]
        xT_32 = [sem(f"xT_32_{i}") for i in range(2)]
        xThi_ready = [sem(f"xThi_ready{i}") for i in range(3)]
        xTlo_ready = [sem(f"xTlo_ready{i}") for i in range(3)]
        lg_ps = [sem(f"lg_ps{i}") for i in range(2)]
        dlt_ready = [sem(f"dlt_ready{i}") for i in range(2)]
        e2_ready = [sem(f"e2_ready{i}") for i in range(2)]
        pos_ps = [sem(f"pos_ps{i}") for i in range(2)]
        wgt_ready = [sem(f"wgt_ready{i}") for i in range(2)]
        wgtT_ps = [sem(f"wgtT_ps{i}") for i in range(2)]
        wgtT_ready = [sem(f"wgtT_ready{i}") for i in range(2)]
        h_ps = [sem(f"h_ps{i}") for i in range(2)]
        h1_ready = [sem(f"h1_ready{i}") for i in range(2)]
        z_ready = [sem(f"z_ready{i}") for i in range(2)]
        silu_ready = [sem(f"silu_ready{i}") for i in range(2)]
        wexp_ps = [sem(f"wexp_ps{i}") for i in range(2)]
        hw_ready = [sem(f"hw_ready{i}") for i in range(2)]
        hThi_ready = [sem(f"hThi_ready{i}") for i in range(2)]
        hTlo_pool = [sem(f"hTlo_pool{i}") for i in range(2)]
        hTlo_dve = [sem(f"hTlo_dve{i}") for i in range(2)]
        y_ps = [sem(f"y_ps{i}") for i in range(2)]
        x_added = [sem(f"x_added{i}") for i in range(3)]
        w_ps = sem("w_ps")
        w_hi = sem("w_hi")
        w_lo = sem("w_lo")
        gate_step = sem("gate_step")
        m_ps = sem("m_ps")
        m_hi = sem("m_hi")
        m_lo = sem("m_lo")
        woT_ps = sem("woT_ps")
        woT_hi = sem("woT_hi")
        woT_lo = sem("woT_lo")
        wuv_hi = sem("wuv_hi")
        wuv_lo = sem("wuv_lo")
        n_ps = sem("n_ps")
        n_hi = sem("n_hi")
        n_lo = sem("n_lo")
        lat_ps = sem("lat_ps")
        lat_hi = sem("lat_hi")
        lat_lo = sem("lat_lo")
        u_ps = sem("u_ps")
        u_hi = sem("u_hi")
        u_lo = sem("u_lo")
        u_moved = [sem(f"u_moved{t}") for t in range(2)]
        s_ps = sem("s_ps")
        max_ready = sem("max_ready")
        prob_ready = sem("prob_ready")
        pT_ps = sem("pT_ps")
        pThi_ready = sem("pThi_ready")
        pTlo_ready = sem("pTlo_ready")
        ctx_ps = sem("ctx_ps")
        rsum_ready = sem("rsum_ready")
        ctx_free = sem("ctx_free")
        cst_ready = sem("cst_ready")
        chi_ready = sem("chi_ready")
        clo_ready = sem("clo_ready")
        chi_last = sem("chi_last")
        clo_last = sem("clo_last")
        cT_ps = sem("cT_ps")
        cThi_ready = sem("cThi_ready")
        cTlo_ready = sem("cTlo_ready")
        attn_ps = sem("attn_ps")
        stored = sem("stored")
        dve_step = sem("dve_step")

        block = ctx.enter_context(nc.Block())

        def weight_splits():
            for n, wT in enumerate((w1T, w3T)):
                for c in range(DC):
                    yield bank[2 * n + c][:, 0:EF], [t[:, c, :] for t in wT]
            yield bank[4][:, 0:2 * D], [t[:, 0:2, :].rearrange("p j d -> p (j d)") for t in w2T]
            yield bank[5][:, 0:D], [t[:, 2, :] for t in w2T]
            src = bank[5][:, D:D + DC * LAT].rearrange("p (c l) -> p c l", c=DC)
            yield src.unsqueeze(2).to_broadcast([P, DC, 2, LAT]), [t[:, :, :, :] for t in wdT]
        N_W = 2 * DC + 3
        GATE_AT = D + DC * LAT

        def tokens(t):
            return slice(t * HALF, (t + 1) * HALF)

        def blk(n):
            return slice(n * P, (n + 1) * P)

        def beyond(i, j):
            return isinstance(i, int) and i * UNITS + j >= NP * UNITS

        @block.sync
        def _(sp):
            sp.dma_start(X[:, 0:HB // 2, :], x_d[:, 0:HB // 2, :]).then_inc(ld["x0"], 16)
            sp.dma_start(w3n[:, :, :], w3.rearrange("e f d -> (e f) d").rearrange("(j p) d -> p j d", p=P)).then_inc(ld["w3"], 16)
            sp.dma_start(gaten[:, :], gate_w).then_inc(ld["gate"], 16)
            for c in range(DC):
                sp.dma_start(w2n[:, c, :].rearrange("p (e f) -> p e f", e=E),
                             w2[:, blk(c), :].rearrange("e p f -> p e f")).then_inc(ld["w2"], 16)
            sp.dma_start(wdn[:, :], W_down).then_inc(ld["wd"], 16)
            sp.dma_start(wq, W_q.rearrange("(h p) d -> p h d", p=P)).then_inc(ld["wq"], 16)
            sp.dma_start(wuk[:, :, :], W_uk.rearrange("(h p) l -> p h l", p=P)).then_inc(ld["wuk"], 16)
            sp.dma_start(wo, W_o.rearrange("(c p) n -> p c n", p=P)).then_inc(ld["wo"], 16)
            sp.dma_start(wuv[:, :, :], W_uv.rearrange("(h p) l -> p h l", p=P)).then_inc(ld["wuv"], 16)

            sp.wait_ge(woT_hi, 8)
            with sp.Fori(0, NP) as i:
                for t in range(2):
                    sp.wait_ge(u_lo, i * 2 + (t + 1))
                    for side in range(2):
                        for part in range(2):
                            sp.dma_start(uc[LAT * part:LAT * (part + 1), bass.ds(i * 2 + side, 1), tokens(t)],
                                         stage[LAT * side:LAT * (side + 1), 0, part:part + 1, tokens(t)]).then_inc(u_moved[t], 16)

            for n in range(NB):
                sp.wait_ge(x_added[2], n + 1)
                sp.dma_start(out_d[:, n, :], X[:, n, :]).then_inc(stored, 16)
            sp.wait_ge(stored, 16 * NB)

        @block.gpsimd
        def _(pool):
            nc.gpsimd.memset(onesb[:, :], 1.0).then_inc(ones_ready, 1)
            nc.gpsimd.memset(ident[:, :], 0.0)
            nc.gpsimd.memset(tri[:, :], 1.0)
            nc.gpsimd.memset(maskneg[:, :], 0.0)
            nc.gpsimd.memset(sel[:, :, :], 0.0)
            nc.gpsimd.memset(lat[:, :, LAT:LAT + 1], 1.0)
            nc.gpsimd.iota(rank_i[:, :, :], pattern=[[0, NB], [-1, E]], base=E, channel_multiplier=0).then_inc(const_step, 1)
            pool.wait_ge(const_step, 1)
            nc.gpsimd.affine_select(out=ident[:, :], in_=ident[:, :], compare_op=ALU.not_equal, fill=1.0,
                                    base=0, pattern=[[-1, P]], channel_multiplier=1)
            nc.gpsimd.affine_select(out=tri[:, :], in_=tri[:, :], compare_op=ALU.is_ge, fill=0.0,
                                    base=0, pattern=[[1, P]], channel_multiplier=-1)
            nc.gpsimd.affine_select(out=maskneg[:, :], in_=maskneg[:, :], compare_op=ALU.is_ge, fill=-1e30,
                                    base=0, pattern=[[-1, P]], channel_multiplier=1)
            nc.gpsimd.tensor_copy(rank[:, :, :], rank_i[:, :, :])
            nc.gpsimd.affine_select(out=sel[:, :, :], in_=sel[:, :, :], compare_op=ALU.not_equal, fill=1.0,
                                    base=0, pattern=[[EPC, FC], [1, EPC], [0, F]], channel_multiplier=-1).then_inc(const_step, 1)
            pool.wait_ge(const_step, 2)
            nc.gpsimd.tensor_copy(identb[:, :], ident[:, :])
            nc.gpsimd.affine_select(out=sel[:, :, :], in_=sel[:, :, :], compare_op=ALU.not_equal, fill=1.0,
                                    base=E, pattern=[[EPC, FC], [1, EPC], [0, F]], channel_multiplier=-1).then_inc(consts, 1)

            def ffn(L):
                for c in range(DC):
                    pool.wait_ge(xT_32[L], c + 1)
                    nc.gpsimd.tensor_tensor(xT_lo[:, c, tokens(0)], xT[:, c, :], xT_hi[:, c, tokens(0)],
                                            ALU.subtract).then_inc(xTlo_ready[2 * L], 1)
                if L == 0:
                    pool.wait_ge(w_lo, N_W + 1)
                    nc.gpsimd.tensor_copy(gate_parts[:, :, 0, :], gateT[:, :, :]).then_inc(gate_step, 1)
                    pool.wait_ge(gate_step, 1)
                    nc.gpsimd.tensor_tensor(gate_rest[:, :, :], gateT[:, :, :], gate_parts[:, :, 0, :], ALU.subtract).then_inc(gate_step, 1)
                    pool.wait_ge(gate_step, 2)
                    nc.gpsimd.tensor_copy(gate_parts[:, :, 1, :], gate_rest[:, :, :]).then_inc(gate_step, 1)
                    pool.wait_ge(gate_step, 3)
                    nc.gpsimd.tensor_tensor(gate_parts[:, :, 2, :], gate_rest[:, :, :], gate_parts[:, :, 1, :], ALU.subtract).then_inc(gate_step, 1)
                for s in (0, 1, 3):
                    t, j = divmod(s, FC)
                    pool.wait_ge(hThi_ready[L], s + 1)
                    nc.gpsimd.tensor_tensor(hT_lo[:, j, tokens(t)], g[:, j, tokens(t)], hT_hi[:, j, tokens(t)],
                                            ALU.subtract).then_inc(hTlo_pool[L], 1)

            ffn(0)
            pool.wait_ge(ld["wuv"], 16)
            nc.gpsimd.tensor_copy(wuv_hl[0][:, :, :], wuv[:, :, :]).then_inc(wuv_hi, 1)
            pool.wait_ge(wuv_hi, 1)
            nc.gpsimd.tensor_tensor(wuv_hl[1][:, :, :], wuv[:, :, :], wuv_hl[0][:, :, :], ALU.subtract).then_inc(wuv_lo, 1)
            pool.wait_ge(n_hi, 4)
            with pool.Fori(0, H - 1) as h:
                for b in range(B):
                    pool.wait_ge(rsum_ready, h * B + (b + 1))
                    pool.wait_ge(ctx_free, h * B + (B + b + 1))
                    nc.gpsimd.tensor_tensor(cst[:, b, :, :], craw[:, b, :, :],
                                            rsum[:, b, :].unsqueeze(2).to_broadcast([P, SB, LAT]), ALU.mult).then_inc(cst_ready, 1)
                    pool.wait_ge(cst_ready, h * B + (b + 1))
                    nc.gpsimd.tensor_copy(c_hi[:, SB * b:SB * (b + 1), bass.ts(h, LAT)], cst[:, b, :, :]).then_inc(chi_ready, 1)
                    pool.wait_ge(chi_ready, h * B + (b + 1))
                    nc.gpsimd.tensor_tensor(c_lo[:, SB * b:SB * (b + 1), bass.ts(h, LAT)], cst[:, b, :, :],
                                            c_hi[:, SB * b:SB * (b + 1), bass.ts(h, LAT)], ALU.subtract).then_inc(clo_ready, 1)
            ffn(1)

        @block.scalar
        def _(act):
            act.dma_start(X[:, HB // 2:HB, :], x_d[:, HB // 2:HB, :]).then_inc(ld["x0"], 16)
            act.dma_start(w1n[:, :, :], w1.rearrange("e f d -> (e f) d").rearrange("(j p) d -> p j d", p=P)).then_inc(ld["w1"], 16)
            act.dma_start(X[:, HB:NB, :], x_d[:, HB:NB, :]).then_inc(ld["x1"], 16)

            def layernorm_std(i, t):
                act.wait_ge(var_ready[i], t + 1)
                half = slice(t * HB, (t + 1) * HB)
                nc.scalar.activation(std[:, half], ve[:, half], ACT.Sqrt).then_inc(std_ready[i], 1)

            def split_xT(L, t):
                for c in range(DC):
                    act.wait_ge(xT_ps[2 * L], DC * t + c + 1)
                    nc.scalar.copy(xT_hi[:, c, tokens(t)], bank[6 - 2 * t + c][:, :]).then_inc(xThi_ready[2 * L], 1)
                if t == 0:
                    for c in range(DC):
                        nc.scalar.copy(xT[:, c, :], bank[6 + c][:, :]).then_inc(xT_32[L], 1)

            def ffn(L):
                def copy_h1(s):
                    act.wait_ge(h_ps[L], s + 1)
                    if s >= 2:
                        act.wait_ge(z_ready[L], s - 1)
                    nc.scalar.copy(h1c[:, s % 2, :], bank[2 * (s % 2)][:, :]).then_inc(h1_ready[L], 1)

                def silu(s):
                    t, j = divmod(s, FC)
                    act.wait_ge(z_ready[L], s + 1)
                    nc.scalar.activation(g[:, j, tokens(t)], g[:, j, tokens(t)], ACT.Silu).then_inc(silu_ready[L], 1)

                def split_h(s):
                    t, j = divmod(s, FC)
                    act.wait_ge(hw_ready[L], s + 1)
                    nc.scalar.copy(hT_hi[:, j, tokens(t)], g[:, j, tokens(t)]).then_inc(hThi_ready[L], 1)

                copy_h1(0)
                split_xT(L, 1)
                copy_h1(1)
                silu(0)
                silu(1)
                act.wait_ge(dlt_ready[L], 1)
                nc.scalar.activation(e2[:, :], dlt[:, :], ACT.Exp).then_inc(e2_ready[L], 1)
                copy_h1(2)
                copy_h1(3)
                silu(2)
                silu(3)
                split_h(0)
                split_h(1)
                copy_h1(4)
                silu(4)
                split_h(2)
                copy_h1(5)
                silu(5)
                for s in range(3, 2 * FC):
                    split_h(s)

            layernorm_std(0, 0)
            for k, (src, dst) in enumerate(weight_splits()):
                act.wait_ge(w_ps, N_W if k >= N_W - 2 else k + 1)
                nc.scalar.copy(dst[0], src).then_inc(w_hi, 1)
                if k == 2 * DC - 1:
                    split_xT(0, 0)
            layernorm_std(0, 1)
            ffn(0)

            layernorm_std(1, 0)
            for k in range(4):
                act.wait_ge(m_ps, k + 1)
                c, hg = divmod(k, 2)
                nc.scalar.activation(Mq[0][:, c, 8 * hg:8 * hg + 8, :].rearrange("p h l -> p (h l)"), bank[4 + k][:, :],
                                     ACT.Copy, scale=SCALE).then_inc(m_hi, 1)
                if k == 0:
                    layernorm_std(1, 1)
            for k in range(2 * DC):
                t, c = divmod(k, DC)
                act.wait_ge(xT_ps[1], k + 1)
                nc.scalar.copy(xT_hi[:, c, tokens(t)], bank[k][:, :]).then_inc(xThi_ready[1], 1)

            def split_woT(k):
                act.wait_ge(woT_ps, k + 1)
                nc.scalar.copy(woT[0][:, 2 * k:2 * k + 2, :].rearrange("p h d -> p (h d)"), bank[4 + k % 3][:, :]).then_inc(woT_hi, 1)

            def split_N(k):
                act.wait_ge(n_ps, k + 1)
                nc.scalar.copy(Nv[0][:, 2 * k:2 * k + 2, :].rearrange("p h d -> p (h d)"), bank[3 + k][:, :]).then_inc(n_hi, 1)

            def split_queries(i, t):
                if not isinstance(i, int):
                    act.wait_ge(u_moved[t], i * 64)
                act.wait_ge(u_ps, i * 2 + (t + 1))
                nc.scalar.copy(stage[:, 0, 0, tokens(t)], bank[7][:, :]).then_inc(u_hi, 1)

            def exponent(i, j):
                u = j % UNITS
                act.wait_ge(max_ready, i * UNITS + (j + 1))
                for n, (b, q, at) in enumerate(HEAD_UNITS[u % HU]):
                    cols = slice(at, at + P * (q + 1))
                    last = nc.scalar.activation(prob[:, u % 2, cols], bank[SCORE_BANK[u]][:, cols], ACT.Exp,
                                                bias=nmax[:, u, n:n + 1])
                last.then_inc(prob_ready, 1)

            def split(i, j):
                act.wait_ge(pT_ps, i * UNITS + (j + 1))
                nc.scalar.copy(pT_hi[:, j % 2, :], bank[3 + j % 2][:, :]).then_inc(pThi_ready, 1)

            def attention_step(i, j, queries=True):
                if not beyond(i, j + 3):
                    exponent(i, j + 3)
                if queries and j in (1, 3):
                    split_queries(i + 1, j // 2)
                if not beyond(i, j + 2):
                    split(i, j + 2)

            for k in range(3):
                split_woT(k)
            split_queries(0, 0)
            for k in range(3, 8):
                split_woT(k)
            for t in range(2):
                act.wait_ge(lat_ps, t + 1)
                nc.scalar.copy(latT_hi[:, tokens(t)], bank[t][:, :]).then_inc(lat_hi, 1)
            split_queries(0, 1)
            act.wait_ge(lat_ps, 3)
            nc.scalar.copy(lat[:, :, 0:LAT], bank[2][:, :].rearrange("p (n l) -> p n l", n=NB)).then_inc(lat_hi, 1)
            for k in range(4):
                split_N(k)
            exponent(0, 0)
            exponent(0, 1)
            split(0, 0)
            exponent(0, 2)
            split(0, 1)
            attention_step(0, 0)
            with act.Fori(0, NP - 1) as i:
                for j in range(1, UNITS + 1):
                    attention_step(i, j)
            for j in range(1, UNITS - 2):
                attention_step(NP - 1, j, queries=False)

            def split_last_context(b):
                act.wait_ge(ctx_free, (H - 1) * B + B + b + 1)
                nc.scalar.copy(c_hi[:, SB * b:SB * (b + 1), (H - 1) * LAT:H * LAT], cst[:, b, :, :]).then_inc(chi_last, 1)

            def context_hi(r, waited):
                act.wait_ge(cT_ps, waited)
                nc.scalar.copy(stage[:, r, 0, :], bank[CTX_T_BANK[r][0]][:, :].bitcast(BF16)).then_inc(cThi_ready, 1)

            split_last_context(0)
            context_hi(0, 1)
            split_last_context(1)
            with act.Fori(0, HB // 2) as i:
                context_hi(1, i * 2 + 2)
                context_hi(0, i * 2 + 3)
            layernorm_std(2, 0)
            for n in range(HB + 1, NB):
                context_hi(n % 2, n + 1)
            split_xT(1, 0)
            layernorm_std(2, 1)
            ffn(1)

        @block.vector
        def _(dve):
            steps = [0]

            def link(ins):
                steps[0] += 1
                ins.then_inc(dve_step, 1)
                dve.wait_ge(dve_step, steps[0])

            def variances(i, t):
                half = range(HB * t, HB * (t + 1))
                if i == 0:
                    dve.wait_ge(ld[f"x{t}"], 16 * (2 - t))
                for n in half:
                    nc.vector.bn_stats(st[:, n, :], X[:, n, :]).then_inc(st_ready, 1)
                aggregate(i, t)

            def statistics(k, n, waited):
                dve.wait_ge(x_added[k], waited)
                nc.vector.bn_stats(st[:, bass.ds(n, 1), :].rearrange("p a s -> p (a s)"),
                                   X[:, bass.ds(n, 1), :].rearrange("p a d -> p (a d)")).then_inc(st_ready, 1)

            def aggregate(i, t):
                half = range(HB * t, HB * (t + 1))
                dve.wait_ge(st_ready, NB * i + HB * (t + 1))
                for n in half:
                    last = nc.vector.bn_aggr(mv[:, n, :], st[:, n, :])
                link(last)
                nc.vector.tensor_scalar_add(ve[:, HB * t:HB * (t + 1)], mv[:, HB * t:HB * (t + 1), 1], EPS).then_inc(var_ready[i], 1)

            def normalise_tokens(i, t):
                dve.wait_ge(std_ready[i], t + 1)
                link(nc.vector.reciprocal(rstd[:, HB * t:HB * (t + 1)], std[:, HB * t:HB * (t + 1)]))
                for n in range(HB * t, HB * (t + 1)):
                    nc.vector.tensor_scalar(xn[:, n, :], X[:, n, :], mv[:, n, 0:1], rstd[:, n:n + 1],
                                            ALU.subtract, ALU.mult).then_inc(xn_ready[i], 1)

            def split_xT(L):
                for c in range(DC):
                    dve.wait_ge(xThi_ready[2 * L], DC + c + 1)
                    nc.vector.tensor_tensor(xT_lo[:, c, tokens(1)], bank[4 + c][:, :], xT_hi[:, c, tokens(1)],
                                            ALU.subtract).then_inc(xTlo_ready[2 * L], 1)

            def split_weights(ks):
                for k, (src, dst) in enumerate(weight_splits()):
                    if k in ks:
                        dve.wait_ge(w_hi, N_W if k >= N_W - 2 else k + 1)
                        nc.vector.tensor_tensor(dst[1], src, dst[0], ALU.subtract).then_inc(w_lo, 1)

            def over_experts(v):
                return v.unsqueeze(2).to_broadcast([P, NB, E])

            def choose(src, k):
                link(nc.vector.reduce_max(top[:, k, :], src, AX.X))
                link(nc.vector.tensor_tensor(eq[:, :, :], src, over_experts(top[:, k, :]), ALU.is_equal))
                link(nc.vector.tensor_tensor(tb[:, :, :], eq[:, :, :], rank[:, :, :], ALU.mult))
                link(nc.vector.reduce_max(tr[:, k, :], tb[:, :, :], AX.X))
                link(nc.vector.tensor_tensor(chosen[:, k, :, :], tb[:, :, :], over_experts(tr[:, k, :]), ALU.is_equal))

            def ffn(L):
                def product(s):
                    t, j = divmod(s, FC)
                    dve.wait_ge(h1_ready[L], s + 1)
                    nc.vector.tensor_tensor(g[:, j, tokens(t)], h1c[:, s % 2, :], bank[2 * (s % 2) + 1][:, :],
                                            ALU.mult).then_inc(z_ready[L], 1)

                def weigh(s):
                    t, j = divmod(s, FC)
                    dve.wait_ge(wexp_ps[L], s + 1)
                    dve.wait_ge(silu_ready[L], s + 1)
                    nc.vector.tensor_tensor(g[:, j, tokens(t)], g[:, j, tokens(t)], bank[5 + 2 * (s % 2)][:, :],
                                            ALU.mult).then_inc(hw_ready[L], 1)

                def split_h(s):
                    t, j = divmod(s, FC)
                    dve.wait_ge(hThi_ready[L], s + 1)
                    nc.vector.tensor_tensor(hT_lo[:, j, tokens(t)], g[:, j, tokens(t)], hT_hi[:, j, tokens(t)],
                                            ALU.subtract).then_inc(hTlo_dve[L], 1)

                product(0)
                product(1)
                dve.wait_ge(lg_ps[L], 1)
                link(nc.vector.tensor_reduce(lg[:, :, :], bank[6][:, 0:NB * 3 * E].rearrange("p (n r e) -> p n e r", n=NB, r=3),
                                             AX.X, ALU.add))
                choose(lg[:, :, :], 0)
                link(nc.vector.tensor_scalar(cp[:, :, :], chosen[:, 0, :, :], -0.5, -2.0 * HUGE, ALU.add, ALU.mult))
                link(nc.vector.tensor_tensor(l2[:, :, :], lg[:, :, :], cp[:, :, :], ALU.min))
                choose(l2[:, :, :], 1)
                nc.vector.tensor_tensor(dlt[:, :], top[:, 1, :], top[:, 0, :], ALU.subtract).then_inc(dlt_ready[L], 1)
                dve.wait_ge(dlt_ready[L], 1)

                dve.wait_ge(e2_ready[L], 1)
                link(nc.vector.tensor_scalar_add(den[:, :], e2[:, :], 1.0))
                link(nc.vector.reciprocal(rec[:, :], den[:, :]))
                nc.vector.tensor_scalar(rw[:, 0, :], rec[:, :], 0.5, None, ALU.mult)
                link(nc.vector.scalar_tensor_tensor(out=rw[:, 1, :], in0=rec[:, :], scalar=0.5, in1=e2[:, :],
                                                    op0=ALU.mult, op1=ALU.mult))
                dve.wait_ge(pos_ps[L], 1)
                link(nc.vector.scalar_tensor_tensor(
                    out=kept[:, :, :, :].rearrange("p s n e -> p (s n e)"), in0=bank[5][:, 0:2 * NB * E],
                    scalar=float(CAP), in1=chosen[:, :, :, :].rearrange("p s n e -> p (s n e)"),
                    op0=ALU.is_le, op1=ALU.mult))
                for k in range(2):
                    last = nc.vector.tensor_tensor(kept[:, k, :, :], kept[:, k, :, :], over_experts(rw[:, k, :]), ALU.mult)
                link(last)
                link(nc.vector.tensor_tensor(wgt[:, :, :], kept[:, 0, :, :], kept[:, 1, :, :], ALU.add))
                link(nc.vector.tensor_copy(wgt_hl[:, :, 0, :], wgt[:, :, :]))
                nc.vector.tensor_tensor(wgt_hl[:, :, 1, :], wgt[:, :, :], wgt_hl[:, :, 0, :],
                                        ALU.subtract).then_inc(wgt_ready[L], 1)
                product(2)
                dve.wait_ge(wgtT_ps[L], 1)
                nc.vector.tensor_copy(wgtT[:, :], bank[6][0:2 * E, :].bitcast(BF16)).then_inc(wgtT_ready[L], 1)
                product(3)
                weigh(0)
                weigh(1)
                product(4)
                weigh(2)
                weigh(3)
                split_h(2)
                product(5)
                weigh(4)
                weigh(5)
                split_h(4)
                split_h(5)
                for n in range(NB):
                    dve.wait_ge(y_ps[L], n + 1)
                    nc.vector.tensor_tensor(X[:, n, :], X[:, n, :], bank[n % 4][:, 0:D], ALU.add).then_inc(x_added[2 * L], 1)
                    if L == 0:
                        if n > 0:
                            statistics(0, n - 1, n)
                        if n == HB:
                            aggregate(1, 0)
                        if n == 6:
                            normalise_tokens(1, 0)

            variances(0, 0)
            normalise_tokens(0, 0)
            split_weights(range(2 * DC))
            variances(0, 1)
            split_weights(range(2 * DC, N_W))
            nc.vector.tensor_copy(gateT[:, :, :], bank[5][:, GATE_AT:GATE_AT + DC * E].rearrange("p (c e) -> p c e", c=DC)).then_inc(w_lo, 1)
            normalise_tokens(0, 1)
            split_xT(0)
            dve.wait_ge(consts, 1)
            ffn(0)

            statistics(0, NB - 1, NB)
            aggregate(1, 1)
            normalise_tokens(1, 1)
            for k in range(4):
                dve.wait_ge(m_hi, k + 1)
                c, hg = divmod(k, 2)
                hi, lo = (m[:, c, 8 * hg:8 * hg + 8, :].rearrange("p h l -> p (h l)") for m in Mq)
                nc.vector.scalar_tensor_tensor(out=lo, in0=bank[4 + k][:, :], scalar=SCALE, in1=hi,
                                               op0=ALU.mult, op1=ALU.subtract).then_inc(m_lo, 1)
            for k in range(2 * DC):
                t, c = divmod(k, DC)
                dve.wait_ge(xThi_ready[1], k + 1)
                nc.vector.tensor_tensor(xT_lo[:, c, tokens(t)], bank[k][:, :], xT_hi[:, c, tokens(t)],
                                        ALU.subtract).then_inc(xTlo_ready[1], 1)

            def split_woT(k):
                dve.wait_ge(woT_hi, k + 1)
                hi, lo = (w[:, 2 * k:2 * k + 2, :].rearrange("p h d -> p (h d)") for w in woT)
                nc.vector.tensor_tensor(lo, bank[4 + k % 3][:, :], hi, ALU.subtract).then_inc(woT_lo, 1)

            def split_N(k):
                dve.wait_ge(n_hi, k + 1)
                hi, lo = (m[:, 2 * k:2 * k + 2, :].rearrange("p h d -> p (h d)") for m in Nv)
                nc.vector.tensor_tensor(lo, bank[3 + k][:, :], hi, ALU.subtract).then_inc(n_lo, 1)

            def split_queries(i, t):
                dve.wait_ge(u_hi, i * 2 + (t + 1))
                nc.vector.tensor_tensor(stage[:, 0, 1, tokens(t)], bank[7][:, :], stage[:, 0, 0, tokens(t)],
                                        ALU.subtract).then_inc(u_lo, 1)

            def row_max(i, j):
                u = j % UNITS
                dve.wait_ge(s_ps, i * UNITS + (j + 1))
                parts = HEAD_UNITS[u % HU]
                src = bank[SCORE_BANK[u]]
                if len({q for _, q, _ in parts}) == 1:
                    last = nc.vector.tensor_reduce(nmax[:, u, 0:len(parts)], src[:, :].rearrange("p (a n) -> p a n", a=len(parts)),
                                                   AX.X, ALU.max, negate=True)
                else:
                    for n, (b, q, at) in enumerate(parts):
                        last = nc.vector.tensor_reduce(nmax[:, u, n:n + 1], src[:, at:at + P * (q + 1)], AX.X, ALU.max, negate=True)
                last.then_inc(max_ready, 1)

            def split(i, j):
                dve.wait_ge(pThi_ready, i * UNITS + (j + 1))
                nc.vector.tensor_tensor(pT_lo[:, j % 2, :], bank[3 + j % 2][:, :], pT_hi[:, j % 2, :],
                                        ALU.subtract).then_inc(pTlo_ready, 1)

            def take_context(i, side, b):
                src = bank[5 + b][:, 0:SB * (LAT + 1)].rearrange("p (q l) -> p q l", q=SB)
                dve.wait_ge(clo_ready, i * (2 * B) + (side * B + 1 + b))
                dve.wait_ge(ctx_ps, i * (2 * B) + (side * B + b + 1))
                nc.vector.reciprocal(rsum[:, b, :], src[:, :, LAT]).then_inc(rsum_ready, 1)
                nc.vector.tensor_copy(craw[:, b, :, :], src[:, :, 0:LAT]).then_inc(ctx_free, 1)

            def normalise_last(b):
                src = bank[5 + b][:, 0:SB * (LAT + 1)].rearrange("p (q l) -> p q l", q=SB)
                dve.wait_ge(clo_ready, (H - 1) * B + 1 + b)
                dve.wait_ge(ctx_ps, (H - 1) * B + b + 1)
                nc.vector.reciprocal(rsum[:, b, :], src[:, :, LAT]).then_inc(rsum_ready, 1)
                dve.wait_ge(rsum_ready, (H - 1) * B + b + 1)
                nc.vector.tensor_tensor(cst[:, b, :, :], src[:, :, 0:LAT],
                                        rsum[:, b, :].unsqueeze(2).to_broadcast([P, SB, LAT]), ALU.mult).then_inc(ctx_free, 1)

            def attention_step(i, j, queries=True):
                side, unit = divmod(j - 1, HU)
                if j and unit in LAST_UNIT:
                    take_context(i, side, LAST_UNIT.index(unit))
                if not beyond(i, j + 1):
                    split(i, j + 1)
                if not beyond(i, j + 4):
                    row_max(i, j + 4)
                if queries and j in (1, 3):
                    split_queries(i + 1, j // 2)

            for k in range(3):
                split_woT(k)
            split_queries(0, 0)
            for k in range(3, 8):
                split_woT(k)
            for t in range(2):
                dve.wait_ge(lat_hi, t + 1)
                nc.vector.tensor_tensor(latT_lo[:, tokens(t)], bank[t][:, :], latT_hi[:, tokens(t)],
                                        ALU.subtract).then_inc(lat_lo, 1)
            split_queries(0, 1)
            dve.wait_ge(lat_hi, 3)
            nc.vector.tensor_tensor(lat[:, :, LAT + 1:2 * LAT + 1], bank[2][:, :].rearrange("p (n l) -> p n l", n=NB),
                                    lat[:, :, 0:LAT], ALU.subtract).then_inc(lat_lo, 1)
            nc.vector.memset(rsum[:, :, :], 0.0).then_inc(ctx_free, B)
            nc.vector.memset(cst[:, :, :, :], 0.0).then_inc(clo_ready, B)
            for k in range(4):
                split_N(k)
            for j in range(4):
                row_max(0, j)
            split(0, 0)
            attention_step(0, 0)
            with dve.Fori(0, NP - 1) as i:
                for j in range(1, UNITS + 1):
                    attention_step(i, j)
            for j in range(1, UNITS - 2):
                attention_step(NP - 1, j, queries=False)

            def split_last_context(b):
                dve.wait_ge(chi_last, b + 1)
                nc.vector.tensor_tensor(c_lo[:, SB * b:SB * (b + 1), (H - 1) * LAT:H * LAT], cst[:, b, :, :],
                                        c_hi[:, SB * b:SB * (b + 1), (H - 1) * LAT:H * LAT], ALU.subtract).then_inc(clo_last, b + 1)

            def context_lo(r, waited):
                dve.wait_ge(cThi_ready, waited)
                nc.vector.tensor_copy(stage[:, r, 1, :], bank[CTX_T_BANK[r][1]][:, :].bitcast(BF16)).then_inc(cTlo_ready, 1)

            def add_attention(r, n, waited):
                dve.wait_ge(attn_ps, waited)
                nc.vector.tensor_tensor(X[:, bass.ds(n, 1), :], X[:, bass.ds(n, 1), :],
                                        bank[OUT_BANK[r]][:, 0:D].unsqueeze(1), ALU.add).then_inc(x_added[1], 1)

            normalise_last(0)
            split(NP - 1, UNITS - 1)
            split_last_context(0)
            context_lo(0, 1)
            normalise_last(1)
            split_last_context(1)

            def two_blocks(i):
                context_lo(1, i * 2 + 2)
                add_attention(0, i * 2, i * 2 + 1)
                context_lo(0, i * 2 + 3)
                statistics(1, i * 2, i * 2 + 1)
                add_attention(1, i * 2 + 1, i * 2 + 2)
                statistics(1, i * 2 + 1, i * 2 + 2)

            with dve.Fori(0, HB // 2) as i:
                two_blocks(i)
            aggregate(2, 0)
            for i in range(HB // 2, NB // 2 - 1):
                two_blocks(i)
            normalise_tokens(2, 0)
            context_lo(1, NB)
            add_attention(0, NB - 2, NB - 1)
            statistics(1, NB - 2, NB - 1)
            add_attention(1, NB - 1, NB)
            statistics(1, NB - 1, NB)
            aggregate(2, 1)
            normalise_tokens(2, 1)
            split_xT(1)
            ffn(1)

        @block.tensor
        def _(pe):
            mm = nc.tensor.matmul

            def split_product(dst, left, right, K, start=True, stop=True):
                terms = [(0, 0, k) for k in range(K)] + [(0, 1, k) for k in range(K)] + [(1, 0, k) for k in range(K)]
                for n, (a, b, k) in enumerate(terms):
                    last = mm(dst, left(k)[a], right(k)[b], start=start and n == 0, stop=stop and n == len(terms) - 1)
                return last

            def transpose_xn(i, t, banks):
                pe.wait_ge(xn_ready[i], HB * (t + 1))
                for c in range(DC):
                    for n in range(HB):
                        last = nc.tensor.transpose(bank[banks + c][:, blk(n)], xn[:, HB * t + n, blk(c)], ident[:, :])
                    last.then_inc(xT_ps[i], 1)

            def ffn(L):
                HIDDEN = [(0, n, w, k) for n in range(2) for w in range(2) for k in range(DC)]
                HI = len(HIDDEN)
                HIDDEN += [(1, n, 0, k) for n in range(2) for k in range(DC)]

                def hidden(s, first=0, until=len(HIDDEN)):
                    t, j = divmod(s, FC)
                    for m in range(first, until):
                        part, n, w, k = HIDDEN[m]
                        if m == 0:
                            pe.wait_ge(xThi_ready[2 * L], DC * (t + 1))
                            if s >= 2:
                                pe.wait_ge(z_ready[L], s - 1)
                        if m == HI:
                            pe.wait_ge(xTlo_ready[2 * L], DC * (t + 1))
                        last = mm(bank[2 * (s % 2) + n][:, :], (w1T, w3T)[n][w][:, k, blk(j)],
                                  (xT_hi, xT_lo)[part][:, k, tokens(t)],
                                  start=(part == 0 and w == 0 and k == 0), stop=(part == 1 and k == DC - 1))
                    if until == len(HIDDEN):
                        last.then_inc(h_ps[L], 1)

                def spread(s):
                    t, j = divmod(s, FC)
                    if s >= 2:
                        pe.wait_ge(hw_ready[L], s - 1)
                    mm(bank[5 + 2 * (s % 2)][:, :], sel[:, j, :], wgtT[:, tokens(t)], start=True, stop=True).then_inc(wexp_ps[L], 1)

                def logits(n):
                    if n % HB == 0:
                        pe.wait_ge(xTlo_ready[2 * L], DC * (n // HB + 1))
                    if n == 0:
                        pe.wait_ge(xT_32[L], DC)
                        pe.wait_ge(gate_step, 4)
                    dst = bank[6][:, n * 3 * E:(n + 1) * 3 * E]
                    parts = [gate_parts[:, c, :, :].rearrange("p r e -> p (r e)") for c in range(DC)]
                    mm(dst, xT_hi[:, 0, blk(n)], parts[0], start=True, stop=False)
                    for c in range(DC):
                        mm(dst[:, 0:2 * E], xT_lo[:, c, blk(n)], parts[c][:, 0:2 * E], start=False, stop=False)
                    for c in range(1, DC):
                        last = mm(dst, xT_hi[:, c, blk(n)], parts[c], start=False, stop=(c == DC - 1))
                    if n == NB - 1:
                        last.then_inc(lg_ps[L], 1)

                def second_half():
                    if L == 0:
                        pe.wait_ge(w_lo, N_W + 1)
                    else:
                        pe.wait_ge(x_added[1], NB)
                    transpose_xn(2 * L, 1, 4)

                def positions():
                    pe.wait_ge(dlt_ready[L], 1)
                    picks = chosen[:, :, :, :].rearrange("p s n e -> p (s n e)")
                    G = 2 * NB
                    mm(bank[5][:, 0:G * E], tri[:, :], picks, start=True, stop=False)
                    for k in range(1, G):
                        last = mm(bank[5][:, k * E:G * E], onesb[:, :], picks[:, 0:(G - k) * E], start=False, stop=(k == G - 1))
                    last.then_inc(pos_ps[L], 1)

                def transpose_weights():
                    pe.wait_ge(wgt_ready[L], 1)
                    for n in range(NB):
                        last = nc.tensor.transpose(bank[6][0:2 * E, :].bitcast(BF16)[:, blk(n)],
                                                   wgt_hl[:, n, :, :].rearrange("p a e -> p (a e)"), identb[:, :])
                    last.then_inc(wgtT_ps[L], 1)

                if L == 0:
                    pe.wait_ge(w_lo, 2 * DC)
                hidden(0)
                hidden(1, 0, 6)
                second_half()
                hidden(1, 6)
                for n in range(NB):
                    logits(n)
                hidden(2)
                hidden(3, 0, 6)
                positions()
                hidden(3, 6)
                transpose_weights()
                hidden(4, 0, 6)
                pe.wait_ge(wgtT_ready[L], 1)
                spread(0)
                spread(1)
                hidden(4, 6)
                hidden(5, 0, 4)
                spread(2)
                spread(3)
                hidden(5, 4)
                spread(4)
                for n in range(NB):
                    t = n // HB
                    if n == 1:
                        spread(5)
                    if n == 2:
                        pe.wait_ge(z_ready[L], 2 * FC)
                    pe.wait_ge(hThi_ready[L], FC * (t + 1))
                    if n >= 4:
                        pe.wait_ge(x_added[2 * L], n - 3)
                    for part, wparts in ((0, (0, 1)), (1, (0,))):
                        if part:
                            pe.wait_ge(hTlo_pool[L], (2, 3)[t])
                            pe.wait_ge(hTlo_dve[L], (1, 3)[t])
                        for w in wparts:
                            for k in range(FC):
                                last = mm(bank[n % 4][:, 0:D], (hT_hi, hT_lo)[part][:, k, blk(n)], w2T[w][:, k, :],
                                          start=(part == 0 and w == 0 and k == 0), stop=(part == 1 and k == FC - 1))
                    last.then_inc(y_ps[L], 1)

            pe.wait_ge(ones_ready, 1)
            for _ in range(12):
                mm(bank[7][:, :], onesb[:, :], onesb[:, :].unsqueeze(1).to_broadcast([P, 512 // P, P]), start=True, stop=True)
            pe.wait_ge(const_step, 2)
            for n, (wn, key) in enumerate(((w1n, "w1"), (w3n, "w3"))):
                pe.wait_ge(ld[key], 16)
                for c in range(DC):
                    for j in range(FC):
                        last = nc.tensor.transpose(bank[2 * n + c][:, blk(j)], wn[:, j, blk(c)], ident[:, :])
                    last.then_inc(w_ps, 1)
            transpose_xn(0, 0, 6)
            pe.wait_ge(ld["w2"], 16 * DC)
            for j in range(FC):
                for c in range(DC):
                    at = (j % 2) * D + c * P
                    last = nc.tensor.transpose(bank[4 + j // 2][:, at:at + P], w2n[:, c, blk(j)], ident[:, :])
                if j >= 1:
                    last.then_inc(w_ps, 1)
            pe.wait_ge(ld["gate"], 16)
            pe.wait_ge(ld["wd"], 16)
            for c in range(DC):
                nc.tensor.transpose(bank[5][:, GATE_AT + c * E:GATE_AT + (c + 1) * E], gaten[:, blk(c)], ident[0:E, 0:E])
            for c in range(DC):
                last = nc.tensor.transpose(bank[5][:, D + c * LAT:D + (c + 1) * LAT], wdn[:, blk(c)], ident[0:LAT, 0:LAT])
            last.then_inc(w_ps, 1)
            ffn(0)

            pe.wait_ge(ld["wq"], 16)
            pe.wait_ge(ld["wuk"], 16)
            for k in range(4):
                c, hg = divmod(k, 2)
                for h in range(8):
                    last = mm(bank[4 + k][:, LAT * h:LAT * (h + 1)], wq[:, 8 * hg + h, blk(c)], wuk[:, 8 * hg + h, :], start=True, stop=True)
                last.then_inc(m_ps, 1)
            pe.wait_ge(x_added[0], NB)
            for t in range(2):
                transpose_xn(1, t, DC * t)
            pe.wait_ge(ld["wo"], 16)

            def transpose_W_o(k):
                if k < 3:
                    pe.wait_ge(m_lo, k + 1)
                else:
                    pe.wait_ge(woT_lo, k - 2)
                for h in range(2):
                    for c in range(DC):
                        at = D * h + P * c
                        last = nc.tensor.transpose(bank[4 + k % 3][:, at:at + P], wo[:, c, blk(2 * k + h)], ident[:, :])
                last.then_inc(woT_ps, 1)

            def queries(i, t):
                if not (isinstance(i, int) and t == 0):
                    pe.wait_ge(u_lo, i * 2 + t)
                split_product(bank[7][:, :],
                              lambda k: [m[:, k, bass.ds(i * 2, 2), :].rearrange("p h l -> p (h l)") for m in Mq],
                              lambda k: [xT_hi[:, k, tokens(t)], xT_lo[:, k, tokens(t)]], DC).then_inc(u_ps, 1)

            def scores(i, j):
                u = j % UNITS
                first_use = {0: 0, 2: 1}
                if u in first_use:
                    pe.wait_ge(u_moved[first_use[u]], i * 64 + 64 * (j // UNITS + 1))
                if HELD_BY[u] is None:
                    if not (isinstance(i, int) and i == NP - 1):
                        pe.wait_ge(u_lo, i * 2 + 4)
                else:
                    held = HELD_BY[u] + j - u
                    if not (isinstance(i, int) and i * UNITS + held < 0):
                        pe.wait_ge(prob_ready, i * UNITS + (held + 1))
                dst = bank[SCORE_BANK[u]]
                for n, (b, q, at) in enumerate(HEAD_UNITS[u % HU]):
                    cols = slice(at, at + P * (q + 1))
                    keys = slice(SEQ * b, SEQ * b + P * (q + 1))
                    queries_of = uc[:, i * 2 + j // HU, SEQ * b + P * q:SEQ * b + P * (q + 1)]
                    mm(dst[:, cols], queries_of, latT_hi[:, keys], start=True, stop=False)
                    mm(dst[:, cols], queries_of, latT_lo[:, keys], start=False, stop=False)
                    last = mm(dst[:, cols][:, P * q:], identb[:, :], maskneg[:, :], start=False, stop=True)
                last.then_inc(s_ps, 1)

            def transposes(i, j):
                pe.wait_ge(prob_ready, i * UNITS + (j + 1))
                if not (isinstance(i, int) and i == 0 and j < 2):
                    pe.wait_ge(pTlo_ready, i * UNITS + (j - 1))
                for k in range(SB):
                    last = nc.tensor.transpose(bank[3 + j % 2][:, blk(k)], prob[:, j % 2, blk(k)], ident[:, :])
                last.then_inc(pT_ps, 1)

            def context(i, j):
                unit = j % HU
                if unit == 0 or unit == 2:
                    pe.wait_ge(ctx_free, i * (2 * B) + (j // HU * B + unit // 2 + 1))
                pe.wait_ge(pTlo_ready, i * UNITS + (j + 1))
                for b, q, at in HEAD_UNITS[unit]:
                    dst = bank[5 + b][:, q * (LAT + 1):(q + 1) * (LAT + 1)]
                    for k in range(q + 1):
                        n = SB * b + k
                        p_hi, p_lo = (p[:, j % 2, at + P * k:at + P * (k + 1)] for p in (pT_hi, pT_lo))
                        mm(dst, p_hi, lat[:, n, 0:LAT + 1], start=(k == 0), stop=False)
                        mm(dst[:, 0:LAT], p_hi, lat[:, n, LAT + 1:2 * LAT + 1], start=False, stop=False)
                        last = mm(dst, p_lo, lat[:, n, 0:LAT + 1], start=False, stop=(k == q))
                if unit in LAST_UNIT:
                    last.then_inc(ctx_ps, 1)

            def attention_step(i, j, with_queries=True):
                if with_queries and j in (1, 3):
                    queries(i + 1, j // 2)
                if not beyond(i, j + 4):
                    scores(i, j + 4)
                context(i, j)
                if not beyond(i, j + 2):
                    transposes(i, j + 2)

            for k in range(3):
                transpose_W_o(k)
            pe.wait_ge(m_lo, 4)
            pe.wait_ge(xTlo_ready[1], DC)
            queries(0, 0)
            for k in range(3, 8):
                transpose_W_o(k)
            for t in range(2):
                pe.wait_ge(xTlo_ready[1], DC * (t + 1))
                split_product(bank[t][:, :],
                              lambda k: [w[:, k, :, :].rearrange("p r l -> p (r l)") for w in wdT],
                              lambda k: [xT_hi[:, k, tokens(t)], xT_lo[:, k, tokens(t)]], DC).then_inc(lat_ps, 1)
            queries(0, 1)
            for n in range(NB):
                last = split_product(bank[2][:, LAT * n:LAT * (n + 1)],
                                     lambda k: [xT_hi[:, k, blk(n)], xT_lo[:, k, blk(n)]],
                                     lambda k: [w[:, k, 0, :] for w in wdT], DC)
            last.then_inc(lat_ps, 1)

            pe.wait_ge(wuv_lo, 1)
            for k in range(4):
                pe.wait_ge(woT_lo, (2, 7, 8, 8)[k])
                for h in range(4):
                    side = h % 2
                    last = split_product(bank[3 + k][LAT * side:LAT * (side + 1), D * (h // 2):D * (h // 2 + 1)],
                                         lambda _: [w[:, 4 * k + h, :] for w in wuv_hl],
                                         lambda _: [w[:, 4 * k + h, :] for w in woT], 1)
                last.then_inc(n_ps, 1)

            pe.wait_ge(lat_lo, 3)
            for j in range(3):
                scores(0, j)
            pe.wait_ge(n_lo, 4)
            transposes(0, 0)
            scores(0, 3)
            transposes(0, 1)
            attention_step(0, 0)
            with pe.Fori(0, NP - 1) as i:
                for j in range(1, UNITS + 1):
                    attention_step(i, j)
            for j in range(1, UNITS - 1):
                attention_step(NP - 1, j, with_queries=False)

            def transpose_context(r, n):
                for part, src in enumerate((c_hi, c_lo)):
                    for k in range(NP):
                        last = nc.tensor.transpose(bank[CTX_T_BANK[r][part]][:, :].bitcast(BF16)[:, blk(k)], src[:, n, blk(k)], identb[:, :])
                last.then_inc(cT_ps, 1)

            def project(r, waited):
                pe.wait_ge(cTlo_ready, waited)
                split_product(bank[OUT_BANK[r]][:, 0:D],
                              lambda k: [stage[:, r, part, blk(k)] for part in range(2)],
                              lambda k: [m[:, k, :] for m in Nv], NP).then_inc(attn_ps, 1)

            pe.wait_ge(clo_ready, B * (H - 1) + 1)
            pe.wait_ge(clo_last, 1)
            transpose_context(0, 0)
            attention_step(NP - 1, UNITS - 1, with_queries=False)
            pe.wait_ge(clo_ready, B * H)

            def two_blocks(i):
                transpose_context(1, i * 2 + 1)
                project(0, i * 2 + 1)
                transpose_context(0, i * 2 + 2)
                project(1, i * 2 + 2)

            with pe.Fori(0, HB // 2) as i:
                pe.wait_ge(clo_last, i + 1)
                two_blocks(i)
            for i in range(HB // 2, NB // 2 - 1):
                two_blocks(i)
            transpose_context(1, NB - 1)
            project(0, NB - 1)
            transpose_xn(2, 0, 6)
            project(1, NB)
            pe.wait_ge(x_added[1], NB - 1)
            ffn(1)


_INS = ['L0_attn_x', 'L0_attn_W_down', 'L0_attn_W_uk', 'L0_attn_W_uv', 'L0_attn_W_q', 'L0_attn_W_o',
        'L0_ffn_gate_w', 'L0_ffn_w1', 'L0_ffn_w2', 'L0_ffn_w3']
_OUTS = [((2, 512, 256), 'float32')]


def kernel(**inputs):
    import numpy as _np
    import concourse.bacc as _bacc
    from concourse import mybir as _mybir
    from concourse.bass_utils import run_bass_kernel_spmd as _run

    nc = _bacc.Bacc("TRN2", target_bir_lowering=False, num_devices=1)
    arrays, args = {}, []
    for name in _INS:
        a = _np.ascontiguousarray(inputs[name])
        arrays[f"in_{name}_dram"] = a
        args.append(nc.dram_tensor(f"in_{name}_dram", a.shape, _mybir.dt.from_np(a.dtype), kind="ExternalInput").ap())
    for i, (shape, dtype) in enumerate(_OUTS):
        dt = _mybir.dt.from_np(_np.dtype(dtype))
        args.append(nc.dram_tensor(f"out_{i}_dram", shape, dt, kind="ExternalOutput").ap())
    bass_macaron_moe_mla_moe(nc, *args)
    r = _run(nc, [arrays], core_ids=[0])
    got = tuple(r.results[0][f"out_{i}_dram"] for i in range(len(_OUTS)))
    return got[0]
```
